# Optimizing a Trainium2 kernel written in Bass

```python
import numpy as np
import jax
import jax.numpy as jnp

def _softmax(x, axis=-1):
    return jax.nn.softmax(x, axis=axis)

def _gelu(x):
    return jax.nn.gelu(x, approximate=True)

def _silu(x):
    return jax.nn.silu(x)

def _sigmoid(x):
    return jax.nn.sigmoid(x)

def _layernorm(x, axis=-1, eps=1e-05):
    m = jnp.mean(x, axis=axis, keepdims=True)
    v = jnp.var(x, axis=axis, keepdims=True)
    return (x - m) / jnp.sqrt(v + eps)

def _scatter_add(tgt, idx, src, axis=0):
    return tgt.at[idx].add(src)

def _segment_sum(src, seg, n):
    return jax.ops.segment_sum(src, seg, n)
kernel_name = 'mk_xattn_seq_d1_seqx_r4_661fa9'

def setup_inputs(seed: int=0):
    np.random.seed(seed)
    _w = jnp.asarray

    def _rec_inputs():
        import jax
        import jax.numpy as jnp
        _rk = jax.random.key(seed)
        x = -0.0002928 + 1 * jax.random.normal(jax.random.fold_in(_rk, 1), (32, 256, 256), jnp.float32)
        _lenS = 256 - jax.random.randint(jax.random.fold_in(_rk, 7), (32,), 0, max(1, 256 // 4) + 1, jnp.int32)
        _lenS2 = 256 - jax.random.randint(jax.random.fold_in(_rk, 8), (32,), 0, max(1, 256 // 4) + 1, jnp.int32)
        _ctx_768P = jax.random.normal(jax.random.fold_in(_rk, 11), (32, 16, 192), jnp.float32)
        _ctx_768c = jax.random.dirichlet(jax.random.fold_in(_rk, 511), 0.3 * jnp.ones((16,), jnp.float32), (32, 256))
        _ctx_768t = jnp.einsum('bsk,bkd->bsd', _ctx_768c, _ctx_768P)
        _ctx_768t = _ctx_768t * jax.lax.rsqrt(jnp.mean(jnp.square(_ctx_768t)) + 1e-12) * 0.953939
        ctx_768 = -0.00423632 + 0.9977 * (_ctx_768t + 0.3 * jax.random.normal(jax.random.fold_in(_rk, 611), (32, 256, 192), jnp.float32))
        return (x, ctx_768)
    x, ctx_768 = _rec_inputs()

    def _L0_xattn_setup():
        import jax, jax.numpy as jnp
        import numpy as np
        DIM, HEADS, DHEAD, CTX_DIM = (256, 16, 64, 192)
        INNER = HEADS * DHEAD
        FF_HID = 4 * DIM
        EPS = 1e-05

        def _ln(x, g, b):
            mu = jnp.mean(x, axis=-1, keepdims=True)
            var = jnp.mean(jnp.square(x - mu), axis=-1, keepdims=True)
            return (x - mu) * jax.lax.rsqrt(var + EPS) * g + b

        def _attn(x, ctx, Wq, Wk, Wv, Wo, bo):
            b, n, _ = x.shape
            m = ctx.shape[1]
            q = (x @ Wq).reshape(b, n, HEADS, DHEAD)
            k = (ctx @ Wk).reshape(b, m, HEADS, DHEAD)
            v = (ctx @ Wv).reshape(b, m, HEADS, DHEAD)
            scale = DHEAD ** (-0.5)
            sim = jnp.einsum('bihd,bjhd->bhij', q, k) * scale
            attn = jax.nn.softmax(sim, axis=-1)
            out = jnp.einsum('bhij,bjhd->bihd', attn, v).reshape(b, n, INNER)
            return out @ Wo + bo
        key = jax.random.key(seed)
        ks = jax.random.split(key, 24)

        def w(k, shape, fan_in):
            return jax.random.normal(k, shape, jnp.float32) * fan_in ** (-0.5)
        inp = {'x': jax.random.normal(ks[0], (2, 512, DIM), jnp.float32), 'context': jax.random.normal(ks[1], (2, 77, CTX_DIM), jnp.float32), 'Wq1': w(ks[2], (DIM, INNER), DIM), 'Wk1': w(ks[3], (DIM, INNER), DIM), 'Wv1': w(ks[4], (DIM, INNER), DIM), 'Wo1': w(ks[5], (INNER, DIM), INNER), 'bo1': jnp.zeros((DIM,), jnp.float32), 'Wq2': w(ks[6], (DIM, INNER), DIM), 'Wk2': w(ks[7], (CTX_DIM, INNER), CTX_DIM), 'Wv2': w(ks[8], (CTX_DIM, INNER), CTX_DIM), 'Wo2': w(ks[9], (INNER, DIM), INNER), 'bo2': jnp.zeros((DIM,), jnp.float32), 'Wp': w(ks[10], (DIM, 2 * FF_HID), DIM), 'bp': jnp.zeros((2 * FF_HID,), jnp.float32), 'W2': w(ks[11], (FF_HID, DIM), FF_HID), 'b2': jnp.zeros((DIM,), jnp.float32), 'g1': jnp.ones((DIM,), jnp.float32), 'be1': jnp.zeros((DIM,), jnp.float32), 'g2': jnp.ones((DIM,), jnp.float32), 'be2': jnp.zeros((DIM,), jnp.float32), 'g3': jnp.ones((DIM,), jnp.float32), 'be3': jnp.zeros((DIM,), jnp.float32)}
        return inp
    _L0_xattn_all = _L0_xattn_setup()
    _L0_xattn_in = {k: v for k, v in _L0_xattn_all.items() if k in ('Wq1', 'Wk1', 'Wv1', 'Wo1', 'bo1', 'Wq2', 'Wk2', 'Wv2', 'Wo2', 'bo2', 'Wp', 'bp', 'W2', 'b2', 'g1', 'be1', 'g2', 'be2', 'g3', 'be3')}
    del _L0_xattn_all
    return {'x': x, 'ctx_768': ctx_768, 'L0_xattn_Wq1': _L0_xattn_in['Wq1'], 'L0_xattn_Wk1': _L0_xattn_in['Wk1'], 'L0_xattn_Wv1': _L0_xattn_in['Wv1'], 'L0_xattn_Wo1': _L0_xattn_in['Wo1'], 'L0_xattn_bo1': _L0_xattn_in['bo1'], 'L0_xattn_Wq2': _L0_xattn_in['Wq2'], 'L0_xattn_Wk2': _L0_xattn_in['Wk2'], 'L0_xattn_Wv2': _L0_xattn_in['Wv2'], 'L0_xattn_Wo2': _L0_xattn_in['Wo2'], 'L0_xattn_bo2': _L0_xattn_in['bo2'], 'L0_xattn_Wp': _L0_xattn_in['Wp'], 'L0_xattn_bp': _L0_xattn_in['bp'], 'L0_xattn_W2': _L0_xattn_in['W2'], 'L0_xattn_b2': _L0_xattn_in['b2'], 'L0_xattn_g1': _L0_xattn_in['g1'], 'L0_xattn_be1': _L0_xattn_in['be1'], 'L0_xattn_g2': _L0_xattn_in['g2'], 'L0_xattn_be2': _L0_xattn_in['be2'], 'L0_xattn_g3': _L0_xattn_in['g3'], 'L0_xattn_be3': _L0_xattn_in['be3']}

def reference(x, ctx_768, L0_xattn_Wq1, L0_xattn_Wk1, L0_xattn_Wv1, L0_xattn_Wo1, L0_xattn_bo1, L0_xattn_Wq2, L0_xattn_Wk2, L0_xattn_Wv2, L0_xattn_Wo2, L0_xattn_bo2, L0_xattn_Wp, L0_xattn_bp, L0_xattn_W2, L0_xattn_b2, L0_xattn_g1, L0_xattn_be1, L0_xattn_g2, L0_xattn_be2, L0_xattn_g3, L0_xattn_be3):
    import jax
    import jax.numpy as jnp

    def _L0_xattn_ref(x, context, Wq1, Wk1, Wv1, Wo1, bo1, Wq2, Wk2, Wv2, Wo2, bo2, Wp, bp, W2, b2, g1, be1, g2, be2, g3, be3):
        import jax, jax.numpy as jnp
        import numpy as np
        DIM, HEADS, DHEAD, CTX_DIM = (256, 16, 64, 192)
        INNER = HEADS * DHEAD
        FF_HID = 4 * DIM
        EPS = 1e-05

        def _ln(x, g, b):
            mu = jnp.mean(x, axis=-1, keepdims=True)
            var = jnp.mean(jnp.square(x - mu), axis=-1, keepdims=True)
            return (x - mu) * jax.lax.rsqrt(var + EPS) * g + b

        def _attn(x, ctx, Wq, Wk, Wv, Wo, bo):
            b, n, _ = x.shape
            m = ctx.shape[1]
            q = (x @ Wq).reshape(b, n, HEADS, DHEAD)
            k = (ctx @ Wk).reshape(b, m, HEADS, DHEAD)
            v = (ctx @ Wv).reshape(b, m, HEADS, DHEAD)
            scale = DHEAD ** (-0.5)
            sim = jnp.einsum('bihd,bjhd->bhij', q, k) * scale
            attn = jax.nn.softmax(sim, axis=-1)
            out = jnp.einsum('bhij,bjhd->bihd', attn, v).reshape(b, n, INNER)
            return out @ Wo + bo
        h = _ln(x, g1, be1)
        x = _attn(h, h, Wq1, Wk1, Wv1, Wo1, bo1) + x
        h = _ln(x, g2, be2)
        x = _attn(h, context, Wq2, Wk2, Wv2, Wo2, bo2) + x
        h = _ln(x, g3, be3)
        y = h @ Wp + bp
        a, gate = (y[..., :FF_HID], y[..., FF_HID:])
        x = a * jax.nn.gelu(gate, approximate=False) @ W2 + b2 + x
        return x
    x = _L0_xattn_ref(x, ctx_768, L0_xattn_Wq1, L0_xattn_Wk1, L0_xattn_Wv1, L0_xattn_Wo1, L0_xattn_bo1, L0_xattn_Wq2, L0_xattn_Wk2, L0_xattn_Wv2, L0_xattn_Wo2, L0_xattn_bo2, L0_xattn_Wp, L0_xattn_bp, L0_xattn_W2, L0_xattn_b2, L0_xattn_g1, L0_xattn_be1, L0_xattn_g2, L0_xattn_be2, L0_xattn_g3, L0_xattn_be3)
    return x

_drawn_inputs = setup_inputs


def setup_inputs(seed=0):
    import zlib

    import numpy as np

    out = dict(_drawn_inputs(seed))
    spreads = {'L0_xattn_bo1': (0.0, 0.1),
     'L0_xattn_bo2': (0.0, 0.1),
     'L0_xattn_bp': (0.0, 0.1),
     'L0_xattn_b2': (0.0, 0.1),
     'L0_xattn_g1': (1.0, 0.2),
     'L0_xattn_be1': (0.0, 0.1),
     'L0_xattn_g2': (1.0, 0.2),
     'L0_xattn_be2': (0.0, 0.368),
     'L0_xattn_g3': (1.0, 0.2),
     'L0_xattn_be3': (0.0, 0.1)}
    factors = {}
    for name, (base, spread) in spreads.items():
        noise = np.random.default_rng([zlib.crc32(name.encode()), seed]).standard_normal(out[name].shape)
        drawn = base * np.exp(spread * noise) if base else spread * noise
        out[name] = jnp.asarray(drawn.astype(out[name].dtype))
    for name, factor in factors.items():
        out[name] = (out[name] * factor).astype(out[name].dtype)
    return out
```

```python
from contextlib import ExitStack

import concourse.bass as bass
from concourse import mybir

F32 = mybir.dt.float32
F32R = mybir.dt.float32r
ALU = mybir.AluOpType
ACT = mybir.ActivationFunctionType
AX_X = mybir.AxisListType.X

P = 128
DIM = 256
KT = DIM // P
SEQ = 256
TT = SEQ // P
HEADS = 16
DHEAD = 64
INNER = HEADS * DHEAD
PAIRS = HEADS // 2
CTX = 192
FF = 4 * DIM
EPS = 1e-5
SCALE = DHEAD ** -0.5

SCORES, WEIGHTED, PROJECTED = 1, 2, 3
FIRST, LOOP, LAST, DRAIN = range(4)


def counts(c):
    return not isinstance(c, int) or c > 0


def sequences(eng, n, step, prepare=None):
    for p in range(PAIRS):
        step(0, p, FIRST)
    with eng.Fori(1, n - 1) as b:
        for p in range(PAIRS):
            step(b, p, LOOP)
    for p in range(PAIRS):
        step(n - 1, p, LAST)
    for p in range(PROJECTED):
        step(n, p, DRAIN)


def alive(part, p, lag):
    return p >= lag if part == FIRST else p < lag if part == DRAIN else True


def make_identity(nc, pool, ident, made):
    pool.memset(ident[:], 0.0).then_inc(made, 1)
    pool.wait_ge(made, 1)
    pool.affine_select(out=ident[:], in_=ident[:], compare_op=ALU.not_equal, fill=1.0, base=0,
                       pattern=[[-1, P]], channel_multiplier=1).then_inc(made, 1)


def attention(nc, tag, x_in, ctx_in, x_out, wq, wk, wv, wo, bo, gamma, beta):
    n = x_in.shape[0]
    cross = ctx_in is not None

    with ExitStack() as es:
        def sb(name, shape, dt):
            return es.enter_context(nc.sbuf_tensor(tag + name, shape, dt))

        def bank(name, banks=1):
            return es.enter_context(nc.psum_tensor(tag + name, [P, banks * 512], F32))

        def sem(name):
            return es.enter_context(nc.semaphore(tag + name))

        raw = {w: sb("raw_" + w, [P, 2048], F32) for w in ("wq", "wk", "wv", "wo")}
        w_hi = {w: sb("hi_" + w, [P, 2048], F32R) for w in ("wq", "wk", "wv", "wo")}
        w_lo = {w: sb("lo_" + w, [P, 2048], F32R) for w in ("wq", "wk", "wv", "wo")}
        by_k = {w: (w_hi[w][:].rearrange("p (k n) -> p k n", k=KT), w_lo[w][:].rearrange("p (k n) -> p k n", k=KT))
                for w in ("wq", "wk", "wv")}
        wo_hi = w_hi["wo"][:].rearrange("p (k n) -> p k n", k=PAIRS)
        wo_lo = w_lo["wo"][:].rearrange("p (k n) -> p k n", k=PAIRS)
        gamma_c = sb("gamma", [P, KT], F32)
        beta_c = sb("beta", [P, KT], F32)
        bo_row = sb("bo", [P, DIM], F32)
        ident = sb("ident", [P, P], F32)
        pause = sb("pause", [P, 1], F32)
        minus_half = sb("minus_half", [P, TT], F32)

        xt = sb("xt", [P, TT, DIM], F32)
        xres = sb("xres", [P, TT, DIM], F32)
        xnorm = sb("xnorm", [P, TT, DIM], F32)
        yout = sb("yout", [P, TT, DIM], F32)
        stats = sb("stats", [P, TT, 6], F32)
        meanvar = sb("meanvar", [P, TT, 2], F32)
        var_eps = sb("var_eps", [P, TT], F32)
        rstd = sb("rstd", [P, TT], F32)
        h_t = sb("h_t", [P, KT, SEQ], F32)
        h_hi = sb("h_hi", [P, KT, SEQ], F32R)
        h_lo = sb("h_lo", [P, KT, SEQ], F32R)
        if cross:
            ct = sb("ct", [P, TT, DIM], F32)
            c_t = sb("c_t", [P, KT, SEQ], F32)
            c_hi = sb("c_hi", [P, KT, SEQ], F32R)
            c_lo = sb("c_lo", [P, SEQ], F32R)
        qk_hi = sb("qk_hi", [P, 2, 2, SEQ], F32R)
        qk_lo = sb("qk_lo", [P, 2, 2, SEQ], F32R)
        v = sb("v", [P, TT, INNER], F32)
        probs = sb("probs", [P, 2, 2, TT, SEQ], F32)
        probs_t = sb("probs_t", [P, 2, TT, SEQ], F32)
        row_max = sb("row_max", [P, 2 * TT], F32)
        neg_max = sb("neg_max", [P, 2 * TT], F32)
        row_sum = sb("row_sum", [P, 2, 2 * TT], F32)
        row_inv = sb("row_inv", [P, 2, 2 * TT], F32)
        o_hi = sb("o_hi", [P, 2, SEQ], F32R)
        o_lo = sb("o_lo", [P, 2, SEQ], F32R)

        ps_qk = bank("ps_qk")
        ps_s = bank("ps_s", 2)
        ps_pt = [bank("ps_pt0"), bank("ps_pt1")]
        ps_o = bank("ps_o")
        ps_y = bank("ps_y")
        ps_misc = bank("ps_misc")
        scores = ps_s[:].rearrange("p (h t k) -> p h t k", h=2, t=TT)

        loaded = {w: sem("loaded_" + w) for w in raw}
        consts_loaded = sem("consts_loaded")
        w_hi_ready = sem("w_hi_ready")
        w_ready = sem("w_ready")
        ident_made = sem("ident_made")
        half_made = sem("half_made")
        x_loaded = sem("x_loaded")
        ctx_loaded = sem("ctx_loaded")
        y_stored = sem("y_stored")
        xres_ready = sem("xres_ready")
        stats_ready = sem("stats_ready")
        meanvar_ready = sem("meanvar_ready")
        var_ready = sem("var_ready")
        rstd_ready = sem("rstd_ready")
        xnorm_ready = sem("xnorm_ready")
        h_transposed = sem("h_transposed")
        h_t_ready = sem("h_t_ready")
        h_hi_ready = sem("h_hi_ready")
        h_ready = sem("h_ready")
        c_transposed = sem("c_transposed")
        c_t_ready = sem("c_t_ready")
        c_hi_ready = sem("c_hi_ready")
        c_ready = sem("c_ready")
        qk_done = sem("qk_done")
        qk_hi_ready = sem("qk_hi_ready")
        qk_ready = sem("qk_ready")
        v_done = sem("v_done")
        v_ready = sem("v_ready")
        scores_done = sem("scores_done")
        max_ready = sem("max_ready")
        neg_max_ready = sem("neg_max_ready")
        exps_done = sem("exps_done")
        inv_ready = sem("inv_ready")
        probs_ready = sem("probs_ready")
        probs_transposed = sem("probs_transposed")
        probs_t_ready = sem("probs_t_ready")
        pv_done = sem("pv_done")
        o_hi_ready = sem("o_hi_ready")
        o_ready = sem("o_ready")
        wo_done = sem("wo_done")
        y_added = sem("y_added")

        def rows(seq):
            return seq.rearrange("(t p) d -> p t d", p=P)

        block = es.enter_context(nc.Block())

        @block.sync
        def _(sp):
            with nc.allow_non_contiguous_dma(reason="columns of 128 scales"):
                sp.dma_start(gamma_c[:], gamma.rearrange("(k p) -> p k", p=P)).then_inc(consts_loaded, 16)
                sp.dma_start(beta_c[:], beta.rearrange("(k p) -> p k", p=P)).then_inc(consts_loaded, 16)

            def load_context(b):
                c = rows(ctx_in[b])
                sp.dma_start(ct[:, :, 0:CTX], c).then_inc(ctx_loaded, 16)
                sp.dma_start(ct[:, :, CTX:DIM], c[:, :, P:CTX]).then_inc(ctx_loaded, 16)

            sp.dma_start(xt[:], rows(x_in[0])).then_inc(x_loaded, 16)
            if cross:
                load_context(0)
            for w, src in (("wq", wq), ("wk", wk), ("wv", wv)):
                if src.shape[0] == DIM:
                    sp.dma_start(raw[w][:].rearrange("p (k n) -> p k n", k=KT),
                                 src.rearrange("(k p) n -> p k n", p=P)).then_inc(loaded[w], 16)
                else:
                    sp.dma_start(raw[w][:, 0:INNER], src[0:P, :]).then_inc(loaded[w], 16)
                    sp.dma_start(raw[w][0:CTX - P, INNER:2 * INNER], src[P:CTX, :]).then_inc(loaded[w], 16)
                    sp.dma_start(raw[w][CTX - P:P, INNER:2 * INNER], src[P:CTX, :]).then_inc(loaded[w], 16)
            sp.dma_start(raw["wo"][:].rearrange("p (k n) -> p k n", k=PAIRS),
                         wo.rearrange("(k p) n -> p k n", p=P)).then_inc(loaded["wo"], 16)
            sp.dma_start(bo_row[:], bo.partition_broadcast(P)).then_inc(consts_loaded, 16)

            def sequence(b, load):
                if load:
                    sp.wait_ge(xnorm_ready, b + 1)
                    sp.wait_ge(xres_ready, b + 1)
                    sp.dma_start(xt[:], rows(x_in[b + 1])).then_inc(x_loaded, 16)
                    if cross:
                        sp.wait_ge(c_transposed, b + 1)
                        load_context(b + 1)

            def store(b):
                sp.wait_ge(y_added, b + 1)
                sp.dma_start(rows(x_out[b]), yout[:]).then_inc(y_stored, 16)

            sequence(0, True)
            with sp.Fori(1, n - 1) as b:
                store(b - 1)
                sequence(b, True)
            store(n - 2)
            store(n - 1)
            sp.wait_ge(y_stored, 16 * n)

        @block.gpsimd
        def _(pool):
            make_identity(nc, pool, ident, ident_made)
            pool.memset(minus_half[:], -0.5).then_inc(half_made, 1)
            pool.wait_ge(half_made, 1)

            def norm_power(b):
                pool.wait_ge(var_ready, b + 1)
                if counts(c := b):
                    pool.wait_ge(xnorm_ready, c)
                pool.tensor_tensor(rstd[:], var_eps[:], minus_half[:], ALU.pow).then_inc(rstd_ready, 1)

            def residual(b):
                pool.wait_ge(x_loaded, 16 * (b + 1))
                if counts(c := b):
                    pool.wait_ge(y_added, c)
                if counts(c := 16 * b):
                    pool.wait_ge(y_stored, c)
                bias = bo_row[:].unsqueeze(1).to_broadcast([P, TT, DIM])
                pool.tensor_tensor(xres[:], xt[:], bias, ALU.add).then_inc(xres_ready, 1)

            norm_power(0)
            pool.wait_ge(consts_loaded, 48)
            residual(0)
            norm_power(1)
            with pool.Fori(1, n - 1) as b:
                residual(b)
                norm_power(b + 1)
            residual(n - 1)

        @block.scalar
        def _(act):
            def step(b, p, part):
                g = PAIRS * b + p
                if alive(part, p, WEIGHTED):
                    for h in range(2):
                        if counts(c := g - WEIGHTED):
                            act.wait_ge(pv_done, c)
                        if counts(c := 2 * (g - WEIGHTED) + h + 1):
                            act.wait_ge(probs_transposed, c)
                        act.activation(probs_t[:, h].rearrange("p t q -> p (t q)"), ps_pt[h][:],
                                       ACT.Copy).then_inc(probs_t_ready, 1)
                if alive(part, p, SCORES):
                    slot = (p - SCORES) % 2
                    act.wait_ge(neg_max_ready, g - SCORES + 1)
                    if counts(c := 2 * (g - SCORES - 1)):
                        act.wait_ge(probs_transposed, c)
                    for h in range(2):
                        for t in range(TT):
                            i = TT * h + t
                            last = act.activation(probs[:, slot, h, t], scores[:, h, t], ACT.Exp,
                                                  bias=neg_max[:, i:i + 1], scale=SCALE,
                                                  accum_out=row_sum[:, slot, i:i + 1])
                        last.then_inc(exps_done, 1)
                if part != DRAIN:
                    act.wait_ge(qk_done, g + 1)
                    if counts(c := g - 1):
                        act.wait_ge(scores_done, c)
                    act.activation(qk_hi[:, p % 2].rearrange("p a q -> p (a q)"), ps_qk[:],
                                   ACT.Copy).then_inc(qk_hi_ready, 1)
                if alive(part, p, WEIGHTED):
                    slot = (p - WEIGHTED) % 2
                    act.wait_ge(pv_done, g - WEIGHTED + 1)
                    if counts(c := g - WEIGHTED - 1):
                        act.wait_ge(wo_done, c)
                    act.activation(o_hi[:, slot], ps_o[:, 0:SEQ],
                                   ACT.Copy).then_inc(o_hi_ready, 1)
                if part != DRAIN and p in V_STEPS:
                    i = V_STEPS.index(p)
                    half, t = divmod(i, TT)
                    act.wait_ge(v_done, 4 * b + i + 1)
                    if counts(c := PAIRS * b if half else PAIRS * b - 4):
                        act.wait_ge(pv_done, c)
                    act.activation(v[:, t, half * 512:(half + 1) * 512], ps_misc[:], ACT.Copy).then_inc(v_ready, 1)

            sequences(act, n, step)

        @block.vector
        def _(dve):
            def norm_stats(b):
                dve.wait_ge(x_loaded, 16 * (b + 1))
                for t in range(TT):
                    nc.vector.bn_stats(stats[:, t], xt[:, t]).then_inc(stats_ready, 1)
                dve.wait_ge(stats_ready, TT * (b + 1))
                nc.vector.memset(pause[:], 0.0)
                for t in range(TT):
                    nc.vector.bn_aggr(meanvar[:, t], stats[:, t]).then_inc(meanvar_ready, 1)
                dve.wait_ge(meanvar_ready, TT * (b + 1))
                nc.vector.tensor_scalar(var_eps[:], meanvar[:, :, 1], EPS, None, ALU.add).then_inc(var_ready, 1)

            def norm_apply(b):
                dve.wait_ge(rstd_ready, b + 1)
                if counts(c := b):
                    dve.wait_ge(h_transposed, c)
                for t in range(TT):
                    last = nc.vector.tensor_scalar(xnorm[:, t], xt[:, t], meanvar[:, t, 0:1], rstd[:, t:t + 1],
                                                   ALU.subtract, ALU.mult)
                last.then_inc(xnorm_ready, 1)

            def scale_shift(b):
                dve.wait_ge(h_transposed, b + 1)
                for k in range(KT):
                    last = nc.vector.tensor_scalar(h_t[:, k], ps_misc[:, k * SEQ:(k + 1) * SEQ], gamma_c[:, k:k + 1],
                                                   beta_c[:, k:k + 1], ALU.mult, ALU.add)
                last.then_inc(h_t_ready, 1)

            def context_copy(b):
                dve.wait_ge(c_transposed, b + 1)
                nc.vector.tensor_copy(c_t[:].rearrange("p k q -> p (k q)"), ps_misc[:]).then_inc(c_t_ready, 1)

            def split_h(b):
                dve.wait_ge(h_t_ready, b + 1)
                if counts(c := PAIRS * b):
                    dve.wait_ge(qk_done, c)
                if counts(c := 4 * b):
                    dve.wait_ge(v_done, c)
                nc.vector.tensor_copy(h_hi[:], h_t[:]).then_inc(h_hi_ready, 1)
                dve.wait_ge(h_hi_ready, b + 1)
                nc.vector.tensor_tensor(h_lo[:], h_t[:], h_hi[:].bitcast(F32), ALU.subtract).then_inc(h_ready, 1)

            def split_context(b):
                dve.wait_ge(c_t_ready, b + 1)
                if counts(c := PAIRS * b):
                    dve.wait_ge(qk_done, c)
                if counts(c := 4 * b):
                    dve.wait_ge(v_done, c)
                nc.vector.tensor_copy(c_hi[:], c_t[:]).then_inc(c_hi_ready, 1)
                dve.wait_ge(c_hi_ready, b + 1)
                nc.vector.tensor_tensor(c_lo[:], c_t[:, 0], c_hi[:, 0].bitcast(F32), ALU.subtract).then_inc(c_ready, 1)
                nc.vector.tensor_tensor(c_hi[64:P, 1], c_t[64:P, 1], c_hi[64:P, 1].bitcast(F32),
                                        ALU.subtract).then_inc(c_ready, 1)

            norm_stats(0)
            norm_apply(0)
            for i, w in enumerate(("wq", "wk", "wv", "wo")):
                if i == 2:
                    dve.wait_ge(consts_loaded, 48)
                    if cross:
                        context_copy(0)
                    scale_shift(0)
                    split_h(0)
                    if cross:
                        split_context(0)
                dve.wait_ge(loaded[w], 48 if cross and w in ("wk", "wv") else 16)
                nc.vector.tensor_copy(w_hi[w][:], raw[w][:]).then_inc(w_hi_ready, 1)
                dve.wait_ge(w_hi_ready, i + 1)
                nc.vector.tensor_tensor(w_lo[w][:], raw[w][:], w_hi[w][:].bitcast(F32),
                                        ALU.subtract).then_inc(w_ready, 1)

            def step(b, p, part):
                g = PAIRS * b + p
                if alive(part, p, SCORES):
                    s = g - SCORES
                    slot = (p - SCORES) % 2
                    dve.wait_ge(scores_done, s + 1)
                    nc.vector.tensor_reduce(row_max[:], ps_s[:].rearrange("p (i k) -> p i k", k=SEQ),
                                            AX_X, ALU.max).then_inc(max_ready, 1)
                    dve.wait_ge(max_ready, s + 1)
                    nc.vector.tensor_scalar(neg_max[:], row_max[:], -SCALE, None, ALU.mult).then_inc(neg_max_ready, 1)
                    for h in range(2):
                        dve.wait_ge(exps_done, 2 * s + h + 1)
                        nc.vector.reciprocal(row_inv[:, slot, TT * h:TT * h + TT],
                                             row_sum[:, slot, TT * h:TT * h + TT]).then_inc(inv_ready, 1)
                        dve.wait_ge(inv_ready, 2 * s + h + 1)
                        for t in range(TT):
                            i = TT * h + t
                            last = nc.vector.tensor_scalar(probs[:, slot, h, t], probs[:, slot, h, t],
                                                           row_inv[:, slot, i:i + 1], None, ALU.mult)
                        last.then_inc(probs_ready, 1)
                if part != DRAIN:
                    dve.wait_ge(qk_hi_ready, g + 1)
                    if counts(c := g - 1):
                        dve.wait_ge(scores_done, c)
                    nc.vector.tensor_tensor(qk_lo[:, p % 2].rearrange("p a q -> p (a q)"), ps_qk[:],
                                            qk_hi[:, p % 2].rearrange("p a q -> p (a q)").bitcast(F32),
                                            ALU.subtract).then_inc(qk_ready, 1)
                if alive(part, p, WEIGHTED):
                    slot = (p - WEIGHTED) % 2
                    dve.wait_ge(o_hi_ready, g - WEIGHTED + 1)
                    if counts(c := g - WEIGHTED - 1):
                        dve.wait_ge(wo_done, c)
                    nc.vector.tensor_tensor(o_lo[:, slot], ps_o[:, 0:SEQ],
                                            o_hi[:, slot].bitcast(F32), ALU.subtract).then_inc(o_ready, 1)
                if p == PROJECTED - 1 and part != FIRST:
                    if counts(c := PAIRS * b):
                        dve.wait_ge(wo_done, c)
                    if counts(c := b):
                        dve.wait_ge(xres_ready, c)
                    nc.vector.tensor_tensor(yout[:].rearrange("p t d -> p (t d)"), ps_y[:],
                                            xres[:].rearrange("p t d -> p (t d)"), ALU.add).then_inc(y_added, 1)
                if part in (FIRST, LOOP):
                    if p == 4:
                        norm_stats(b + 1)
                    if p == 5:
                        norm_apply(b + 1)
                        if cross:
                            context_copy(b + 1)
                    if p == 6:
                        scale_shift(b + 1)
                    if p == 7:
                        split_h(b + 1)
                        if cross:
                            split_context(b + 1)

            sequences(dve, n, step)

        @block.tensor
        def _(pe):
            def terms(source_h, w):
                hi, lo = by_k[w]
                if source_h:
                    for k in range(KT):
                        yield h_hi[:, k], hi[:, k]
                        yield h_lo[:, k], hi[:, k]
                        yield h_hi[:, k], lo[:, k]
                else:
                    yield c_hi[:, 0], hi[:, 0]
                    yield c_lo[:], hi[:, 0]
                    yield c_hi[:, 0], lo[:, 0]
                    yield c_hi[:, 1], hi[:, 1]
                    yield c_hi[:, 1], lo[:, 1]

            def project_pair(out, p, source_h, w):
                passes = list(terms(source_h, w))
                for i, (a, m) in enumerate(passes):
                    last = nc.tensor.matmul(out, m[:, p * P:(p + 1) * P], a, start=i == 0, stop=i == len(passes) - 1)
                return last

            def transposes(src, done):
                for k in range(KT):
                    for t in range(TT):
                        last = nc.tensor.transpose(ps_misc[:, k * SEQ + t * P:k * SEQ + (t + 1) * P],
                                                   src[:, t, k * P:(k + 1) * P], ident[:])
                last.then_inc(done, 1)

            def transpose_h(b):
                pe.wait_ge(xnorm_ready, b + 1)
                if counts(c := 4 * b):
                    pe.wait_ge(v_ready, c)
                if cross:
                    pe.wait_ge(c_t_ready, b + 1)
                transposes(xnorm, h_transposed)

            def transpose_context(b):
                pe.wait_ge(ctx_loaded, 32 * (b + 1))
                if counts(c := 4 * b):
                    pe.wait_ge(v_ready, c)
                transposes(ct, c_transposed)

            def step(b, p, part):
                g = PAIRS * b + p
                if alive(part, p, SCORES):
                    s = g - SCORES
                    slot = (p - SCORES) % 2
                    pe.wait_ge(qk_ready, s + 1)
                    if counts(c := 2 * s):
                        pe.wait_ge(exps_done, c)
                    for t in range(TT):
                        for i, (a, m) in enumerate(((qk_hi, qk_hi), (qk_lo, qk_hi), (qk_hi, qk_lo))):
                            for h in range(2):
                                r = slice(DHEAD * h, DHEAD * (h + 1))
                                last = nc.tensor.matmul(scores[:, h, t], a[r, slot, 0, t * P:(t + 1) * P],
                                                        m[r, slot, 1], start=i == 0, stop=i == 2)
                    last.then_inc(scores_done, 1)
                if alive(part, p, WEIGHTED):
                    s = g - WEIGHTED
                    slot = (p - WEIGHTED) % 2
                    for h in range(2):
                        pe.wait_ge(probs_ready, 2 * s + h + 1)
                        if counts(c := 2 * (s - 1) + h + 1):
                            pe.wait_ge(probs_t_ready, c)
                        for k in range(TT):
                            for t in range(TT):
                                last = nc.tensor.transpose(ps_pt[h][:, k * SEQ + t * P:k * SEQ + (t + 1) * P],
                                                           probs[:, slot, h, t, k * P:(k + 1) * P], ident[:])
                        last.then_inc(probs_transposed, 1)
                if part != DRAIN:
                    pe.wait_ge(h_ready, b + 1)
                    if cross:
                        pe.wait_ge(c_ready, 2 * (b + 1))
                    if counts(c := g):
                        pe.wait_ge(qk_ready, c)
                    project_pair(ps_qk[:, 0:SEQ], p, True, "wq")
                    project_pair(ps_qk[:, SEQ:2 * SEQ], p, not cross, "wk").then_inc(qk_done, 1)
                if alive(part, p, WEIGHTED):
                    s = g - WEIGHTED
                    q = (p - WEIGHTED) % PAIRS
                    seq = b if p >= WEIGHTED else b - 1
                    pe.wait_ge(v_ready, 4 * seq + (2 if q < 4 else 4))
                    if counts(c := s):
                        pe.wait_ge(o_ready, c)
                    if counts(c := 2 * s + 2):
                        pe.wait_ge(probs_t_ready, c)
                    for k in range(TT):
                        for h in range(2):
                            c = (2 * q + h) * DHEAD
                            last = nc.tensor.matmul(
                                ps_o[DHEAD * h:DHEAD * (h + 1), 0:SEQ],
                                v[:, k, c:c + DHEAD], probs_t[:, h, k], start=k == 0, stop=k == TT - 1)
                    last.then_inc(pv_done, 1)
                if alive(part, p, PROJECTED):
                    s = g - PROJECTED
                    q = (p - PROJECTED) % PAIRS
                    pe.wait_ge(o_ready, s + 1)
                    if q == 0:
                        if counts(c := b):
                            pe.wait_ge(y_added, c)
                    for t in range(TT):
                        for i, (a, m) in enumerate(((o_hi, wo_hi), (o_lo, wo_hi), (o_hi, wo_lo))):
                            last = nc.tensor.matmul(ps_y[:, t * DIM:(t + 1) * DIM], a[:, q % 2, t * P:(t + 1) * P],
                                                    m[:, q], start=q == 0 and t == 0 and i == 0,
                                                    stop=q == PAIRS - 1 and t == TT - 1 and i == 2,
                                                    skip_group_check=True)
                    last.then_inc(wo_done, 1)
                if part != DRAIN and p in V_STEPS:
                    i = V_STEPS.index(p)
                    half, t = divmod(i, TT)
                    if counts(c := 4 * b + i):
                        pe.wait_ge(v_ready, c)
                    passes = list(terms(not cross, "wv"))
                    for j, (a, m) in enumerate(passes):
                        last = nc.tensor.matmul(ps_misc[:], a[:, t * P:(t + 1) * P], m[:, half * 512:(half + 1) * 512],
                                                start=j == 0, stop=j == len(passes) - 1)
                    last.then_inc(v_done, 1)
                if part in (FIRST, LOOP):
                    if p == 5 and cross:
                        transpose_context(b + 1)
                    if p == 6:
                        transpose_h(b + 1)

            pe.wait_ge(ident_made, 2)
            if cross:
                transpose_context(0)
            transpose_h(0)
            pe.wait_ge(w_ready, 4)
            sequences(pe, n, step)


V_STEPS = (0, 1, 3, 4)

GROUP = 2
GT = GROUP * TT
GTOK = GROUP * SEQ
HT = FF // P
DOWN = 2


def feed_forward(nc, tag, x_in, x_out, wp, bp, w2, b2, gamma, beta):
    n = x_in.shape[0] // GROUP

    with ExitStack() as es:
        def sb(name, shape, dt):
            return es.enter_context(nc.sbuf_tensor(tag + name, shape, dt))

        def bank(name, banks=1):
            return es.enter_context(nc.psum_tensor(tag + name, [P, banks * 512], F32))

        def sem(name):
            return es.enter_context(nc.semaphore(tag + name))

        wp_raw = sb("wp_raw", [P, KT, 2 * FF], F32)
        wp_hi = sb("wp_hi", [P, KT, 2 * FF], F32R)
        wp_lo = sb("wp_lo", [P, KT, 2 * FF], F32R)
        w2_raw = sb("w2_raw", [P, HT, DIM], F32)
        w2_hi = sb("w2_hi", [P, HT, DIM], F32R)
        w2_lo = sb("w2_lo", [P, HT, DIM], F32R)
        bp_c = sb("bp", [P, 2 * HT], F32)
        b2_row = sb("b2", [P, DIM], F32)
        gamma_c = sb("gamma", [P, KT], F32)
        beta_c = sb("beta", [P, KT], F32)
        ident = sb("ident", [P, P], F32)
        pause = sb("pause", [P, 1], F32)
        minus_half = sb("minus_half", [P, GT], F32)
        xt = sb("xt", [P, GT, DIM], F32)
        xres = sb("xres", [P, GT, DIM], F32)
        xnorm = sb("xnorm", [P, GT, DIM], F32)
        yout = sb("yout", [P, GT, DIM], F32)
        stats = sb("stats", [P, GT, 6], F32)
        meanvar = sb("meanvar", [P, GT, 2], F32)
        var_eps = sb("var_eps", [P, GT], F32)
        rstd = sb("rstd", [P, GT], F32)
        h_t = sb("h_t", [P, KT, GTOK], F32)
        h_hi = sb("h_hi", [P, KT, GTOK], F32R)
        h_lo = sb("h_lo", [P, KT, GTOK], F32R)
        gelu = sb("gelu", [P, 2, GTOK], F32)
        gated = sb("gated", [P, 2, GTOK], F32)
        u_hi = sb("u_hi", [P, 2, GTOK], F32R)
        u_lo = sb("u_lo", [P, 2, GTOK], F32R)

        ps_gate = [bank("ps_gate0"), bank("ps_gate1")]
        ps_a = [bank("ps_a0"), bank("ps_a1")]
        ps_y = bank("ps_y", 2)
        ps_ht = bank("ps_ht", 2)

        wp_loaded = sem("wp_loaded")
        w2_loaded = sem("w2_loaded")
        consts_loaded = sem("consts_loaded")
        w_hi_ready = sem("w_hi_ready")
        w_ready = sem("w_ready")
        ident_made = sem("ident_made")
        half_made = sem("half_made")
        x_loaded = sem("x_loaded")
        y_stored = sem("y_stored")
        xres_ready = sem("xres_ready")
        stats_ready = sem("stats_ready")
        meanvar_ready = sem("meanvar_ready")
        var_ready = sem("var_ready")
        rstd_ready = sem("rstd_ready")
        xnorm_ready = sem("xnorm_ready")
        h_transposed = sem("h_transposed")
        h_t_ready = sem("h_t_ready")
        h_hi_ready = sem("h_hi_ready")
        h_ready = sem("h_ready")
        gate_done = sem("gate_done")
        a_done = sem("a_done")
        gelu_ready = sem("gelu_ready")
        gated_ready = sem("gated_ready")
        u_hi_ready = sem("u_hi_ready")
        u_ready = sem("u_ready")
        down_done = sem("down_done")
        y_added = sem("y_added")

        x_in = x_in.rearrange("(n s) q d -> n (s q) d", s=GROUP)
        x_out = x_out.rearrange("(n s) q d -> n (s q) d", s=GROUP)

        def rows(group):
            return group.rearrange("(t p) d -> p t d", p=P)

        def groups(eng, step):
            for j in range(HT):
                step(0, j, FIRST)
            with eng.Fori(1, n - 1) as b:
                for j in range(HT):
                    step(b, j, LOOP)
            for j in range(HT):
                step(n - 1, j, LAST)
            for j in range(DOWN):
                step(n, j, DRAIN)

        block = es.enter_context(nc.Block())

        @block.sync
        def _(sp):
            with nc.allow_non_contiguous_dma(reason="columns of 128 scales"):
                sp.dma_start(gamma_c[:], gamma.rearrange("(k p) -> p k", p=P)).then_inc(consts_loaded, 16)
                sp.dma_start(beta_c[:], beta.rearrange("(k p) -> p k", p=P)).then_inc(consts_loaded, 16)
                sp.dma_start(bp_c[:], bp.rearrange("(k p) -> p k", p=P)).then_inc(consts_loaded, 16)
            sp.dma_start(b2_row[:], b2.partition_broadcast(P)).then_inc(consts_loaded, 16)
            sp.dma_start(xt[:], rows(x_in[0])).then_inc(x_loaded, 16)
            sp.dma_start(wp_raw[:], wp.rearrange("(k p) n -> p k n", p=P)).then_inc(wp_loaded, 16)
            sp.dma_start(w2_raw[:], w2.rearrange("(k p) n -> p k n", p=P)).then_inc(w2_loaded, 16)

            def load(b):
                if counts(c := b):
                    sp.wait_ge(xnorm_ready, c)
                if counts(c := b):
                    sp.wait_ge(xres_ready, c)
                sp.dma_start(xt[:], rows(x_in[b])).then_inc(x_loaded, 16)

            def store(b):
                sp.wait_ge(y_added, 2 * (b + 1))
                sp.dma_start(rows(x_out[b]), yout[:]).then_inc(y_stored, 16)

            load(1)
            with sp.Fori(1, n - 1) as b:
                store(b - 1)
                load(b + 1)
            store(n - 2)
            store(n - 1)
            sp.wait_ge(y_stored, 16 * n)

        @block.gpsimd
        def _(pool):
            make_identity(nc, pool, ident, ident_made)
            pool.memset(minus_half[:], -0.5).then_inc(half_made, 1)
            pool.wait_ge(half_made, 1)

            def norm_power(b):
                pool.wait_ge(var_ready, b + 1)
                if counts(c := b):
                    pool.wait_ge(xnorm_ready, c)
                pool.tensor_tensor(rstd[:], var_eps[:], minus_half[:], ALU.pow).then_inc(rstd_ready, 1)

            def residual(b):
                pool.wait_ge(x_loaded, 16 * (b + 1))
                if counts(c := 2 * b):
                    pool.wait_ge(y_added, c)
                if counts(c := 16 * b):
                    pool.wait_ge(y_stored, c)
                bias = b2_row[:].unsqueeze(1).to_broadcast([P, GT, DIM])
                pool.tensor_tensor(xres[:], xt[:], bias, ALU.add).then_inc(xres_ready, 1)

            norm_power(0)
            pool.wait_ge(consts_loaded, 64)
            residual(0)
            norm_power(1)
            with pool.Fori(1, n - 1) as b:
                residual(b)
                norm_power(b + 1)
            residual(n - 1)

        @block.scalar
        def _(act):
            act.wait_ge(consts_loaded, 64)

            def step(b, j, part):
                if part == DRAIN:
                    return
                i = HT * b + j
                slot = j % 2
                act.wait_ge(gate_done, i + 1)
                if counts(c := i - 1):
                    act.wait_ge(gated_ready, c)
                act.activation(gelu[:, slot], ps_gate[slot][:], ACT.Gelu,
                               bias=bp_c[:, HT + j:HT + j + 1]).then_inc(gelu_ready, 1)
                act.wait_ge(gated_ready, i + 1)
                if counts(c := i - 1):
                    act.wait_ge(down_done, c)
                act.activation(u_hi[:, slot], gated[:, slot], ACT.Copy).then_inc(u_hi_ready, 1)

            groups(act, step)

        @block.vector
        def _(dve):
            def norm_stats(b):
                dve.wait_ge(x_loaded, 16 * (b + 1))
                for t in range(GT):
                    nc.vector.bn_stats(stats[:, t], xt[:, t]).then_inc(stats_ready, 1)
                dve.wait_ge(stats_ready, GT * (b + 1))
                nc.vector.memset(pause[:], 0.0)
                for t in range(GT):
                    nc.vector.bn_aggr(meanvar[:, t], stats[:, t]).then_inc(meanvar_ready, 1)
                dve.wait_ge(meanvar_ready, GT * (b + 1))
                nc.vector.tensor_scalar(var_eps[:], meanvar[:, :, 1], EPS, None, ALU.add).then_inc(var_ready, 1)

            def norm_apply(b):
                dve.wait_ge(rstd_ready, b + 1)
                if counts(c := b):
                    dve.wait_ge(h_transposed, c)
                for t in range(GT):
                    last = nc.vector.tensor_scalar(xnorm[:, t], xt[:, t], meanvar[:, t, 0:1], rstd[:, t:t + 1],
                                                   ALU.subtract, ALU.mult)
                last.then_inc(xnorm_ready, 1)

            def scale_shift(b):
                dve.wait_ge(h_transposed, b + 1)
                for k in range(KT):
                    last = nc.vector.tensor_scalar(h_t[:, k], ps_ht[:, k * GTOK:(k + 1) * GTOK], gamma_c[:, k:k + 1],
                                                   beta_c[:, k:k + 1], ALU.mult, ALU.add)
                last.then_inc(h_t_ready, 1)

            def split_h(b):
                dve.wait_ge(h_t_ready, b + 1)
                if counts(c := HT * b):
                    dve.wait_ge(a_done, c)
                for k in range(KT):
                    nc.vector.tensor_copy(h_hi[:, k], h_t[:, k]).then_inc(h_hi_ready, 1)
                for k in range(KT):
                    dve.wait_ge(h_hi_ready, KT * b + k + 1)
                    nc.vector.tensor_tensor(h_lo[:, k], h_t[:, k], h_hi[:, k].bitcast(F32),
                                            ALU.subtract).then_inc(h_ready, 1)

            norm_stats(0)
            norm_apply(0)
            dve.wait_ge(consts_loaded, 64)
            scale_shift(0)
            split_h(0)
            for i, (loaded, raw, hi, lo) in enumerate(((wp_loaded, wp_raw, wp_hi, wp_lo),
                                                       (w2_loaded, w2_raw, w2_hi, w2_lo))):
                dve.wait_ge(loaded, 16)
                nc.vector.tensor_copy(hi[:], raw[:]).then_inc(w_hi_ready, 1)
                dve.wait_ge(w_hi_ready, i + 1)
                nc.vector.tensor_tensor(lo[:], raw[:], hi[:].bitcast(F32), ALU.subtract).then_inc(w_ready, 1)

            def step(b, j, part):
                i = HT * b + j
                slot = j % 2
                if part != DRAIN:
                    dve.wait_ge(a_done, i + 1)
                    dve.wait_ge(gelu_ready, i + 1)
                    if counts(c := i - 1):
                        dve.wait_ge(u_ready, c)
                    if counts(c := i - 1):
                        dve.wait_ge(u_hi_ready, c)
                    nc.vector.scalar_tensor_tensor(gated[:, slot], ps_a[slot][:], bp_c[:, j:j + 1], gelu[:, slot],
                                                   ALU.add, ALU.mult).then_inc(gated_ready, 1)
                    dve.wait_ge(u_hi_ready, i + 1)
                    if counts(c := i - 1):
                        dve.wait_ge(down_done, c)
                    nc.vector.tensor_tensor(u_lo[:, slot], gated[:, slot], u_hi[:, slot].bitcast(F32),
                                            ALU.subtract).then_inc(u_ready, 1)
                if j == DOWN - 1 and part != FIRST:
                    if counts(c := HT * b):
                        dve.wait_ge(down_done, c)
                    if counts(c := b):
                        dve.wait_ge(xres_ready, c)
                    for half in range(2):
                        r = slice(half * TT, (half + 1) * TT)
                        nc.vector.tensor_tensor(yout[:, r].rearrange("p t d -> p (t d)"),
                                                ps_y[:, half * 512:(half + 1) * 512],
                                                xres[:, r].rearrange("p t d -> p (t d)"),
                                                ALU.add).then_inc(y_added, 1)
                if part in (FIRST, LOOP):
                    if j == 4:
                        norm_stats(b + 1)
                    if j == 5:
                        norm_apply(b + 1)
                    if j == 6:
                        scale_shift(b + 1)
                    if j == 7:
                        split_h(b + 1)

            groups(dve, step)

        @block.tensor
        def _(pe):
            def transpose_h(b):
                pe.wait_ge(xnorm_ready, b + 1)
                if counts(c := b):
                    pe.wait_ge(h_t_ready, c)
                for k in range(KT):
                    for t in range(GT):
                        last = nc.tensor.transpose(ps_ht[:, k * GTOK + t * P:k * GTOK + (t + 1) * P],
                                                   xnorm[:, t, k * P:(k + 1) * P], ident[:])
                last.then_inc(h_transposed, 1)

            def up(out, column, done):
                passes = [t for k in range(KT) for t in ((wp_hi, h_hi, k), (wp_hi, h_lo, k), (wp_lo, h_hi, k))]
                for i, (w, h, k) in enumerate(passes):
                    last = nc.tensor.matmul(out, w[:, k, column:column + P], h[:, k], start=i == 0, stop=i == 5)
                last.then_inc(done, 1)

            def step(b, j, part):
                i = HT * b + j
                slot = j % 2
                if part != DRAIN:
                    pe.wait_ge(h_ready, KT * (b + 1))
                    if counts(c := i - 1):
                        pe.wait_ge(gelu_ready, c)
                    up(ps_gate[slot][:], FF + j * P, gate_done)
                    if counts(c := i - 1):
                        pe.wait_ge(gated_ready, c)
                    up(ps_a[slot][:], j * P, a_done)
                if alive(part, j, DOWN):
                    q = (j - DOWN) % HT
                    pe.wait_ge(u_ready, i - DOWN + 1)
                    if q == 0:
                        if counts(c := 2 * b):
                            pe.wait_ge(y_added, c)
                    for t in range(GT):
                        for s, (a, m) in enumerate(((u_hi, w2_hi), (u_lo, w2_hi), (u_hi, w2_lo))):
                            last = nc.tensor.matmul(ps_y[:, t * DIM:(t + 1) * DIM], a[:, q % 2, t * P:(t + 1) * P],
                                                    m[:, q], start=q == 0 and t % 2 == 0 and s == 0,
                                                    stop=q == HT - 1 and t % 2 == 1 and s == 2,
                                                    skip_group_check=True)
                    last.then_inc(down_done, 1)
                if part in (FIRST, LOOP) and j == 6:
                    transpose_h(b + 1)

            pe.wait_ge(ident_made, 2)
            transpose_h(0)
            pe.wait_ge(w_ready, 2)
            groups(pe, step)


_W = "L0_xattn_"
_INS = ["x", "ctx_768"] + [_W + w for w in (
    "Wq1", "Wk1", "Wv1", "Wo1", "bo1", "Wq2", "Wk2", "Wv2", "Wo2", "bo2", "Wp", "bp", "W2", "b2",
    "g1", "be1", "g2", "be2", "g3", "be3")]


def block_program(nc, a, out):
    x1 = nc.dram_tensor("after_self_attention", a["x"].shape, F32).ap()
    x2 = nc.dram_tensor("after_cross_attention", a["x"].shape, F32).ap()
    w = {k[len(_W):]: v for k, v in a.items() if k.startswith(_W)}
    attention(nc, "self_", a["x"], None, x1, w["Wq1"], w["Wk1"], w["Wv1"], w["Wo1"], w["bo1"], w["g1"], w["be1"])
    attention(nc, "cross_", x1, a["ctx_768"], x2, w["Wq2"], w["Wk2"], w["Wv2"], w["Wo2"], w["bo2"],
              w["g2"], w["be2"])
    feed_forward(nc, "ff_", x2, out, w["Wp"], w["bp"], w["W2"], w["b2"], w["g3"], w["be3"])


def kernel(**inputs):
    import numpy as np
    import concourse.bacc as bacc
    from concourse.bass_utils import run_bass_kernel_spmd

    nc = bacc.Bacc("TRN2", target_bir_lowering=False, num_devices=1)
    arrays, aps = {}, {}
    for name in _INS:
        arrays["in_" + name] = np.ascontiguousarray(inputs[name])
        aps[name] = nc.dram_tensor("in_" + name, arrays["in_" + name].shape, F32, kind="ExternalInput").ap()
    out = nc.dram_tensor("out", arrays["in_x"].shape, F32, kind="ExternalOutput").ap()
    block_program(nc, aps, out)
    r = run_bass_kernel_spmd(nc, [arrays], core_ids=[0])
    return r.results[0]["out"]
```

```python
from contextlib import ExitStack

import concourse.bass as bass
from concourse import mybir

F32 = mybir.dt.float32
F32R = mybir.dt.float32r
ALU = mybir.AluOpType
ACT = mybir.ActivationFunctionType
AX_X = mybir.AxisListType.X

P = 128
DIM = 256
KT = DIM // P
SEQ = 256
TT = SEQ // P
HEADS = 16
DHEAD = 64
INNER = HEADS * DHEAD
PAIRS = HEADS // 2
CTX = 192
FF = 4 * DIM
EPS = 1e-5
SCALE = DHEAD ** -0.5

SCORES, TRANSPOSED, WEIGHTED, PROJECTED = 1, 2, 3, 4
FIRST, LOOP, LAST, DRAIN = range(4)


def counts(c):
    return not isinstance(c, int) or c > 0


def sequences(eng, n, step, prepare=None):
    for p in range(PAIRS):
        step(0, p, FIRST)
    with eng.Fori(1, n - 1) as b:
        for p in range(PAIRS):
            step(b, p, LOOP)
    for p in range(PAIRS):
        step(n - 1, p, LAST)
    for p in range(PROJECTED):
        step(n, p, DRAIN)


def alive(part, p, lag):
    return p >= lag if part == FIRST else p < lag if part == DRAIN else True


def make_identity(nc, pool, ident, made):
    pool.memset(ident[:], 0.0).then_inc(made, 1)
    pool.wait_ge(made, 1)
    pool.affine_select(out=ident[:], in_=ident[:], compare_op=ALU.not_equal, fill=1.0, base=0,
                       pattern=[[-1, P]], channel_multiplier=1).then_inc(made, 1)


WEIGHTS = ("wq", "wk", "wv", "wo")
W_COLS = KT * INNER


class AttentionWeights:

    def __init__(self, buffer, loaded, sources, prefetched):
        self.buffer, self.loaded, self.prefetched = buffer, loaded, prefetched
        self.sources = dict(zip(WEIGHTS, sources))

    def raw(self, w):
        i = WEIGHTS.index(w)
        return self.buffer[:, i * W_COLS:(i + 1) * W_COLS]

    def count(self, w):
        return 48 if self.sources[w].shape[0] == CTX else 16

    def load(self, sp):
        for w, src in self.sources.items():
            dst = self.raw(w)
            if src.shape[0] == CTX:
                sp.dma_start(dst[:, 0:INNER], src[0:P, :]).then_inc(self.loaded[w], 16)
                sp.dma_start(dst[0:CTX - P, INNER:], src[P:CTX, :]).then_inc(self.loaded[w], 16)
                sp.dma_start(dst[CTX - P:P, INNER:], src[P:CTX, :]).then_inc(self.loaded[w], 16)
            else:
                sp.dma_start(dst.rearrange("p (k n) -> p k n", n=src.shape[1]),
                             src.rearrange("(k p) n -> p k n", p=P)).then_inc(self.loaded[w], 16)


class FeedForwardWeights:

    def __init__(self, buffer, loaded, wp, w2):
        self.loaded, self.wp, self.w2 = loaded, wp, w2
        self.raw_wp = buffer[:, 0:2 * W_COLS].rearrange("p (k n) -> p k n", k=KT)
        self.raw_w2 = buffer[:, 2 * W_COLS:3 * W_COLS].rearrange("p (k n) -> p k n", n=DIM)

    def load(self, sp):
        sp.dma_start(self.raw_wp, self.wp.rearrange("(k p) n -> p k n", p=P)).then_inc(self.loaded["wp"], 16)
        sp.dma_start(self.raw_w2, self.w2.rearrange("(k p) n -> p k n", p=P)).then_inc(self.loaded["w2"], 16)


def attention(nc, tag, x_in, ctx_in, x_out, weights, bo, gamma, beta, prefetch):
    n = x_in.shape[0]
    cross = ctx_in is not None

    with ExitStack() as es:
        def sb(name, shape, dt):
            return es.enter_context(nc.sbuf_tensor(tag + name, shape, dt))

        def bank(name, banks=1):
            return es.enter_context(nc.psum_tensor(tag + name, [P, banks * 512], F32))

        def sem(name):
            return es.enter_context(nc.semaphore(tag + name))

        w_hi = {w: sb("hi_" + w, [P, W_COLS], F32R) for w in WEIGHTS}
        w_lo = {w: sb("lo_" + w, [P, W_COLS], F32R) for w in WEIGHTS}
        by_k = {w: (w_hi[w][:].rearrange("p (k n) -> p k n", k=KT), w_lo[w][:].rearrange("p (k n) -> p k n", k=KT))
                for w in ("wq", "wk", "wv")}
        wo_hi = w_hi["wo"][:].rearrange("p (k n) -> p k n", k=PAIRS)
        wo_lo = w_lo["wo"][:].rearrange("p (k n) -> p k n", k=PAIRS)
        gamma_c = sb("gamma", [P, KT], F32)
        beta_c = sb("beta", [P, KT], F32)
        bo_row = sb("bo", [P, DIM], F32)
        ident = sb("ident", [P, P], F32)
        pause = sb("pause", [P, 1], F32)
        minus_half = sb("minus_half", [P, TT], F32)

        xt = sb("xt", [P, TT, DIM], F32)
        xres = sb("xres", [P, TT, DIM], F32)
        xnorm = sb("xnorm", [P, TT, DIM], F32)
        yout = sb("yout", [P, TT, DIM], F32)
        stats = sb("stats", [P, TT, 6], F32)
        meanvar = sb("meanvar", [P, TT, 2], F32)
        var_eps = sb("var_eps", [P, TT], F32)
        rstd = sb("rstd", [P, TT], F32)
        h_t = sb("h_t", [P, KT, SEQ], F32)
        h_hi = sb("h_hi", [P, KT, SEQ], F32R)
        h_lo = sb("h_lo", [P, KT, SEQ], F32R)
        if cross:
            ct = sb("ct", [P, TT, DIM], F32)
            c_t = sb("c_t", [P, KT, SEQ], F32)
            c_hi = sb("c_hi", [P, KT, SEQ], F32R)
            c_lo = sb("c_lo", [P, SEQ], F32R)
        qk_hi = sb("qk_hi", [P, 2, 2, SEQ], F32R)
        qk_lo = sb("qk_lo", [P, 2, 2, SEQ], F32R)
        v = sb("v", [P, TT, INNER], F32)
        probs = sb("probs", [P, 2, 2, TT, SEQ], F32)
        probs_t = sb("probs_t", [P, 2, 2, TT, SEQ], F32)
        row_max = sb("row_max", [P, 2 * TT], F32)
        neg_max = sb("neg_max", [P, 2 * TT], F32)
        row_sum = sb("row_sum", [P, 2, 2 * TT], F32)
        row_inv = sb("row_inv", [P, 2, 2 * TT], F32)
        o_hi = sb("o_hi", [P, 2, SEQ], F32R)
        o_lo = sb("o_lo", [P, 2, SEQ], F32R)

        ps_qk = bank("ps_qk")
        ps_s = bank("ps_s", 2)
        ps_pt = [bank("ps_pt0"), bank("ps_pt1")]
        ps_o = bank("ps_o")
        ps_y = bank("ps_y")
        ps_misc = bank("ps_misc")
        scores = ps_s[:].rearrange("p (h t k) -> p h t k", h=2, t=TT)

        consts_loaded = sem("consts_loaded")
        w_hi_ready = sem("w_hi_ready")
        w_ready = sem("w_ready")
        ident_made = sem("ident_made")
        half_made = sem("half_made")
        x_loaded = sem("x_loaded")
        ctx_loaded = sem("ctx_loaded")
        y_stored = sem("y_stored")
        xres_ready = sem("xres_ready")
        stats_ready = sem("stats_ready")
        meanvar_ready = sem("meanvar_ready")
        var_ready = sem("var_ready")
        rstd_ready = sem("rstd_ready")
        xnorm_ready = sem("xnorm_ready")
        h_transposed = sem("h_transposed")
        h_t_ready = sem("h_t_ready")
        h_hi_ready = sem("h_hi_ready")
        h_ready = sem("h_ready")
        c_transposed = sem("c_transposed")
        c_t_ready = sem("c_t_ready")
        c_hi_ready = sem("c_hi_ready")
        c_ready = sem("c_ready")
        qk_done = sem("qk_done")
        qk_hi_ready = sem("qk_hi_ready")
        qk_ready = sem("qk_ready")
        v_done = sem("v_done")
        v_ready = sem("v_ready")
        scores_done = sem("scores_done")
        max_ready = sem("max_ready")
        neg_max_ready = sem("neg_max_ready")
        exps_done = sem("exps_done")
        inv_ready = sem("inv_ready")
        probs_ready = sem("probs_ready")
        probs_transposed = sem("probs_transposed")
        probs_t_ready = sem("probs_t_ready")
        pv_done = sem("pv_done")
        o_hi_ready = sem("o_hi_ready")
        o_ready = sem("o_ready")
        wo_done = sem("wo_done")
        y_added = sem("y_added")

        def rows(seq):
            return seq.rearrange("(t p) d -> p t d", p=P)

        block = es.enter_context(nc.Block())

        @block.sync
        def _(sp):
            def load_context(b):
                c = rows(ctx_in[b])
                sp.dma_start(ct[:, :, 0:CTX], c).then_inc(ctx_loaded, 16)
                sp.dma_start(ct[:, :, CTX:DIM], c[:, :, P:CTX]).then_inc(ctx_loaded, 16)

            sp.dma_start(xt[:], rows(x_in[0])).then_inc(x_loaded, 16)
            if cross:
                load_context(0)
            if not weights.prefetched:
                weights.load(sp)

            def load_next(b):
                sp.wait_ge(xnorm_ready, b + 1)
                sp.wait_ge(xres_ready, b + 1)
                sp.dma_start(xt[:], rows(x_in[b + 1])).then_inc(x_loaded, 16)
                if cross:
                    sp.wait_ge(c_transposed, b + 1)
                    load_context(b + 1)

            def store(b):
                sp.wait_ge(y_added, b + 1)
                sp.dma_start(rows(x_out[b]), yout[:]).then_inc(y_stored, 16)

            load_next(0)
            prefetch(sp)
            with sp.Fori(1, n - 1) as b:
                store(b - 1)
                load_next(b)
            store(n - 2)
            store(n - 1)
            sp.wait_ge(y_stored, 16 * n)

        @block.gpsimd
        def _(pool):
            make_identity(nc, pool, ident, ident_made)
            pool.memset(minus_half[:], -0.5).then_inc(half_made, 1)
            pool.wait_ge(half_made, 1)

            def norm_power(b):
                pool.wait_ge(var_ready, b + 1)
                if counts(c := b):
                    pool.wait_ge(xnorm_ready, c)
                if counts(c := 16 * (b - 1)):
                    pool.wait_ge(y_stored, c)
                pool.tensor_tensor(rstd[:], var_eps[:], minus_half[:], ALU.pow).then_inc(rstd_ready, 1)

            def residual(b):
                pool.wait_ge(x_loaded, 16 * (b + 1))
                if counts(c := b):
                    pool.wait_ge(y_added, c)
                bias = bo_row[:].unsqueeze(1).to_broadcast([P, TT, DIM])
                pool.tensor_tensor(xres[:], xt[:], bias, ALU.add).then_inc(xres_ready, 1)

            def low_h(b):
                pool.wait_ge(h_hi_ready, b + 1)
                pool.tensor_tensor(h_lo[:], h_t[:], h_hi[:].bitcast(F32), ALU.subtract).then_inc(h_ready, 1)

            norm_power(0)
            low_h(0)
            pool.wait_ge(consts_loaded, 48)
            residual(0)
            norm_power(1)
            low_h(1)
            with pool.Fori(1, n - 1) as b:
                residual(b)
                norm_power(b + 1)
                low_h(b + 1)
            residual(n - 1)

        @block.scalar
        def _(act):
            with nc.allow_non_contiguous_dma(reason="columns of 128 scales"):
                act.dma_start(gamma_c[:], gamma.rearrange("(k p) -> p k", p=P)).then_inc(consts_loaded, 16)
                act.dma_start(beta_c[:], beta.rearrange("(k p) -> p k", p=P)).then_inc(consts_loaded, 16)
            act.dma_start(bo_row[:], bo.partition_broadcast(P)).then_inc(consts_loaded, 16)

            def weight_high(w):
                act.wait_ge(weights.loaded[w], weights.count(w))
                act.activation(w_hi[w][:], weights.raw(w), ACT.Copy).then_inc(w_hi_ready, 1)

            def exps(s, slot, h):
                act.wait_ge(neg_max_ready, s + 1)
                if counts(c := 2 * (s - 1)):
                    act.wait_ge(probs_transposed, c)
                for t in range(TT):
                    i = TT * h + t
                    last = act.activation(probs[:, slot, h, t], scores[:, h, t], ACT.Exp, bias=neg_max[:, i:i + 1],
                                          scale=SCALE, accum_out=row_sum[:, slot, i:i + 1])
                last.then_inc(exps_done, 1)

            def scale_shift(b):
                act.wait_ge(h_transposed, b + 1)
                if counts(c := b):
                    act.wait_ge(h_ready, c)
                for k in range(KT):
                    last = act.activation(h_t[:, k], ps_misc[:, k * SEQ:(k + 1) * SEQ], ACT.Identity,
                                          bias=beta_c[:, k:k + 1], scale=gamma_c[:, k:k + 1])
                last.then_inc(h_t_ready, 1)

            def step(b, p, part):
                g = PAIRS * b + p
                if part != DRAIN:
                    act.wait_ge(qk_done, g + 1)
                    if counts(c := g - 1):
                        act.wait_ge(scores_done, c)
                    act.activation(qk_hi[:, p % 2].rearrange("p a q -> p (a q)"), ps_qk[:],
                                   ACT.Copy).then_inc(qk_hi_ready, 1)
                if alive(part, p, TRANSPOSED):
                    s = g - TRANSPOSED
                    slot = (p - TRANSPOSED) % 2
                    for h in range(2):
                        act.wait_ge(probs_transposed, 2 * s + h + 1)
                        if counts(c := s - 1):
                            act.wait_ge(pv_done, c)
                        act.activation(probs_t[:, slot, h].rearrange("p t q -> p (t q)"), ps_pt[h][:],
                                       ACT.Copy).then_inc(probs_t_ready, 1)
                if alive(part, p, SCORES):
                    for h in range(2):
                        exps(g - SCORES, (p - SCORES) % 2, h)
                if alive(part, p, WEIGHTED):
                    slot = (p - WEIGHTED) % 2
                    act.wait_ge(pv_done, g - WEIGHTED + 1)
                    if counts(c := g - WEIGHTED - 1):
                        act.wait_ge(wo_done, c)
                    act.activation(o_hi[:, slot], ps_o[:, 0:SEQ], ACT.Copy).then_inc(o_hi_ready, 1)
                if part != DRAIN and p in V_STEPS:
                    i = V_STEPS.index(p)
                    half, t = divmod(i, TT)
                    act.wait_ge(v_done, 4 * b + i + 1)
                    if counts(c := PAIRS * b if half else PAIRS * b - 4):
                        act.wait_ge(pv_done, c)
                    act.activation(v[:, t, half * 512:(half + 1) * 512], ps_misc[:], ACT.Copy).then_inc(v_ready, 1)
                if part in (FIRST, LOOP) and p == 6:
                    scale_shift(b + 1)

            weight_high("wq")
            weight_high("wk")
            act.wait_ge(consts_loaded, 48)
            scale_shift(0)
            weight_high("wv")
            weight_high("wo")
            sequences(act, n, step)

        @block.vector
        def _(dve):
            def norm_stats(b):
                dve.wait_ge(x_loaded, 16 * (b + 1))
                for t in range(TT):
                    nc.vector.bn_stats(stats[:, t], xt[:, t]).then_inc(stats_ready, 1)
                dve.wait_ge(stats_ready, TT * (b + 1))
                nc.vector.memset(pause[:], 0.0)
                for t in range(TT):
                    nc.vector.bn_aggr(meanvar[:, t], stats[:, t]).then_inc(meanvar_ready, 1)
                dve.wait_ge(meanvar_ready, TT * (b + 1))
                nc.vector.tensor_scalar(var_eps[:], meanvar[:, :, 1], EPS, None, ALU.add).then_inc(var_ready, 1)

            def norm_apply(b):
                dve.wait_ge(rstd_ready, b + 1)
                if counts(c := b):
                    dve.wait_ge(h_transposed, c)
                for t in range(TT):
                    last = nc.vector.tensor_scalar(xnorm[:, t], xt[:, t], meanvar[:, t, 0:1], rstd[:, t:t + 1],
                                                   ALU.subtract, ALU.mult)
                last.then_inc(xnorm_ready, 1)

            def context_copy(b):
                dve.wait_ge(c_transposed, b + 1)
                nc.vector.tensor_copy(c_t[:].rearrange("p k q -> p (k q)"), ps_misc[:]).then_inc(c_t_ready, 1)

            def high_h(b):
                dve.wait_ge(h_t_ready, b + 1)
                if counts(c := PAIRS * b):
                    dve.wait_ge(qk_done, c)
                if counts(c := 4 * b):
                    dve.wait_ge(v_done, c)
                nc.vector.tensor_copy(h_hi[:], h_t[:]).then_inc(h_hi_ready, 1)

            def high_context(b):
                dve.wait_ge(c_t_ready, b + 1)
                if counts(c := PAIRS * b):
                    dve.wait_ge(qk_done, c)
                if counts(c := 4 * b):
                    dve.wait_ge(v_done, c)
                nc.vector.tensor_copy(c_hi[:], c_t[:]).then_inc(c_hi_ready, 1)

            def low_context(b):
                dve.wait_ge(c_hi_ready, b + 1)
                nc.vector.tensor_tensor(c_lo[:], c_t[:, 0], c_hi[:, 0].bitcast(F32), ALU.subtract).then_inc(c_ready, 1)
                nc.vector.tensor_tensor(c_hi[64:P, 1], c_t[64:P, 1], c_hi[64:P, 1].bitcast(F32),
                                        ALU.subtract).then_inc(c_ready, 1)

            norm_stats(0)
            norm_apply(0)
            for i, w in enumerate(WEIGHTS):
                if w == "wv":
                    if cross:
                        context_copy(0)
                        high_context(0)
                        low_context(0)
                    high_h(0)
                dve.wait_ge(w_hi_ready, i + 1)
                nc.vector.tensor_tensor(w_lo[w][:], weights.raw(w), w_hi[w][:].bitcast(F32),
                                        ALU.subtract).then_inc(w_ready, 1)

            def extras(b, p, part):
                if p == PROJECTED - 1 and part != FIRST:
                    dve.wait_ge(wo_done, PAIRS * b)
                    dve.wait_ge(xres_ready, b)
                    if part == DRAIN:
                        dve.wait_ge(y_stored, 16 * (n - 1))
                    nc.vector.tensor_tensor(yout[:].rearrange("p t d -> p (t d)"), ps_y[:],
                                            xres[:].rearrange("p t d -> p (t d)"), ALU.add).then_inc(y_added, 1)
                if part in (FIRST, LOOP):
                    if p == 4:
                        norm_stats(b + 1)
                    if p == 5:
                        norm_apply(b + 1)
                    if p == 6 and cross:
                        context_copy(b + 1)
                    if p == 7 and cross:
                        low_context(b + 1)

            def step(b, p, part):
                g = PAIRS * b + p
                if part in (FIRST, LOOP) and p == 7:
                    high_h(b + 1)
                    if cross:
                        high_context(b + 1)
                if part != DRAIN:
                    dve.wait_ge(qk_hi_ready, g + 1)
                    if counts(c := g - 1):
                        dve.wait_ge(scores_done, c)
                    nc.vector.tensor_tensor(qk_lo[:, p % 2].rearrange("p a q -> p (a q)"), ps_qk[:],
                                            qk_hi[:, p % 2].rearrange("p a q -> p (a q)").bitcast(F32),
                                            ALU.subtract).then_inc(qk_ready, 1)
                if alive(part, p, SCORES):
                    s = g - SCORES
                    dve.wait_ge(scores_done, s + 1)
                    nc.vector.tensor_reduce(row_max[:], ps_s[:].rearrange("p (i k) -> p i k", k=SEQ),
                                            AX_X, ALU.max).then_inc(max_ready, 1)
                    dve.wait_ge(max_ready, s + 1)
                    nc.vector.tensor_scalar(neg_max[:], row_max[:], -SCALE, None, ALU.mult).then_inc(neg_max_ready, 1)
                extras(b, p, part)
                if alive(part, p, SCORES):
                    s = g - SCORES
                    slot = (p - SCORES) % 2
                    for h in range(2):
                        dve.wait_ge(exps_done, 2 * s + h + 1)
                        nc.vector.reciprocal(row_inv[:, slot, TT * h:TT * h + TT],
                                             row_sum[:, slot, TT * h:TT * h + TT]).then_inc(inv_ready, 1)
                        dve.wait_ge(inv_ready, 2 * s + h + 1)
                        for t in range(TT):
                            i = TT * h + t
                            last = nc.vector.tensor_scalar(probs[:, slot, h, t], probs[:, slot, h, t],
                                                           row_inv[:, slot, i:i + 1], None, ALU.mult)
                        last.then_inc(probs_ready, 1)
                if alive(part, p, WEIGHTED):
                    slot = (p - WEIGHTED) % 2
                    dve.wait_ge(o_hi_ready, g - WEIGHTED + 1)
                    if counts(c := g - WEIGHTED - 1):
                        dve.wait_ge(wo_done, c)
                    nc.vector.tensor_tensor(o_lo[:, slot], ps_o[:, 0:SEQ], o_hi[:, slot].bitcast(F32),
                                            ALU.subtract).then_inc(o_ready, 1)

            sequences(dve, n, step)

        @block.tensor
        def _(pe):
            def terms(source_h, w):
                hi, lo = by_k[w]
                if source_h:
                    for k in range(KT):
                        yield h_hi[:, k], hi[:, k]
                        yield h_lo[:, k], hi[:, k]
                        yield h_hi[:, k], lo[:, k]
                else:
                    yield c_hi[:, 0], hi[:, 0]
                    yield c_lo[:], hi[:, 0]
                    yield c_hi[:, 0], lo[:, 0]
                    yield c_hi[:, 1], hi[:, 1]
                    yield c_hi[:, 1], lo[:, 1]

            def project_pair(out, p, source_h, w):
                passes = list(terms(source_h, w))
                for i, (a, m) in enumerate(passes):
                    last = nc.tensor.matmul(out, m[:, p * P:(p + 1) * P], a, start=i == 0, stop=i == len(passes) - 1)
                return last

            def transposes(src, done):
                for k in range(KT):
                    for t in range(TT):
                        last = nc.tensor.transpose(ps_misc[:, k * SEQ + t * P:k * SEQ + (t + 1) * P],
                                                   src[:, t, k * P:(k + 1) * P], ident[:])
                last.then_inc(done, 1)

            def transpose_h(b):
                pe.wait_ge(xnorm_ready, b + 1)
                if counts(c := 4 * b):
                    pe.wait_ge(v_ready, c)
                if cross:
                    pe.wait_ge(c_t_ready, b + 1)
                transposes(xnorm, h_transposed)

            def transpose_context(b):
                pe.wait_ge(ctx_loaded, 32 * (b + 1))
                if counts(c := 4 * b):
                    pe.wait_ge(v_ready, c)
                transposes(ct, c_transposed)

            def step(b, p, part):
                g = PAIRS * b + p
                if part != DRAIN:
                    pe.wait_ge(h_ready, b + 1)
                    if cross:
                        pe.wait_ge(c_ready, 2 * (b + 1))
                    if counts(c := g):
                        pe.wait_ge(qk_ready, c)
                    project_pair(ps_qk[:, 0:SEQ], p, True, "wq")
                    project_pair(ps_qk[:, SEQ:2 * SEQ], p, not cross, "wk").then_inc(qk_done, 1)
                if alive(part, p, SCORES):
                    s = g - SCORES
                    slot = (p - SCORES) % 2
                    pe.wait_ge(qk_ready, s + 1)
                    if counts(c := 2 * s):
                        pe.wait_ge(exps_done, c)
                    for t in range(TT):
                        for i, (a, m) in enumerate(((qk_hi, qk_hi), (qk_lo, qk_hi), (qk_hi, qk_lo))):
                            for h in range(2):
                                r = slice(DHEAD * h, DHEAD * (h + 1))
                                last = nc.tensor.matmul(scores[:, h, t], a[r, slot, 0, t * P:(t + 1) * P],
                                                        m[r, slot, 1], start=i == 0, stop=i == 2)
                    last.then_inc(scores_done, 1)
                if alive(part, p, TRANSPOSED):
                    s = g - TRANSPOSED
                    slot = (p - TRANSPOSED) % 2
                    for h in range(2):
                        pe.wait_ge(probs_ready, 2 * s + h + 1)
                        if counts(c := 2 * (s - 1) + h + 1):
                            pe.wait_ge(probs_t_ready, c)
                        for k in range(TT):
                            for t in range(TT):
                                last = nc.tensor.transpose(ps_pt[h][:, k * SEQ + t * P:k * SEQ + (t + 1) * P],
                                                           probs[:, slot, h, t, k * P:(k + 1) * P], ident[:])
                        last.then_inc(probs_transposed, 1)
                if alive(part, p, WEIGHTED):
                    s = g - WEIGHTED
                    q = (p - WEIGHTED) % PAIRS
                    seq = b if p >= WEIGHTED else b - 1
                    pe.wait_ge(v_ready, 4 * seq + (2 if q < 4 else 4))
                    if counts(c := s):
                        pe.wait_ge(o_ready, c)
                    if counts(c := 2 * s + 2):
                        pe.wait_ge(probs_t_ready, c)
                    for k in range(TT):
                        for h in range(2):
                            c = (2 * q + h) * DHEAD
                            last = nc.tensor.matmul(
                                ps_o[DHEAD * h:DHEAD * (h + 1), 0:SEQ],
                                v[:, k, c:c + DHEAD], probs_t[:, q % 2, h, k], start=k == 0, stop=k == TT - 1)
                    last.then_inc(pv_done, 1)
                if alive(part, p, PROJECTED):
                    s = g - PROJECTED
                    q = (p - PROJECTED) % PAIRS
                    pe.wait_ge(o_ready, s + 1)
                    if part == FIRST and q == 0:
                        pe.wait_ge(w_ready, 4)
                    if q == 0:
                        if counts(c := b):
                            pe.wait_ge(y_added, c)
                    for t in range(TT):
                        for i, (a, m) in enumerate(((o_hi, wo_hi), (o_lo, wo_hi), (o_hi, wo_lo))):
                            last = nc.tensor.matmul(ps_y[:, t * DIM:(t + 1) * DIM], a[:, q % 2, t * P:(t + 1) * P],
                                                    m[:, q], start=q == 0 and t == 0 and i == 0,
                                                    stop=q == PAIRS - 1 and t == TT - 1 and i == 2,
                                                    skip_group_check=True)
                    last.then_inc(wo_done, 1)
                if part != DRAIN and p in V_STEPS:
                    i = V_STEPS.index(p)
                    half, t = divmod(i, TT)
                    if counts(c := 4 * b + i):
                        pe.wait_ge(v_ready, c)
                    if part == FIRST and i == 0:
                        pe.wait_ge(w_ready, 3)
                    passes = list(terms(not cross, "wv"))
                    for j, (a, m) in enumerate(passes):
                        last = nc.tensor.matmul(ps_misc[:], a[:, t * P:(t + 1) * P], m[:, half * 512:(half + 1) * 512],
                                                start=j == 0, stop=j == len(passes) - 1)
                    last.then_inc(v_done, 1)
                if part in (FIRST, LOOP):
                    if p == 5 and cross:
                        transpose_context(b + 1)
                    if p == 6:
                        transpose_h(b + 1)

            pe.wait_ge(ident_made, 2)
            if cross:
                transpose_context(0)
            transpose_h(0)
            pe.wait_ge(w_ready, 2)
            sequences(pe, n, step)


V_STEPS = (0, 1, 3, 4)

GROUP = 2
GT = GROUP * TT
GTOK = GROUP * SEQ
HT = FF // P
WP_PARTS = (slice(FF, FF + 512), slice(0, 512), slice(FF + 512, 2 * FF), slice(512, FF))
DOWN = 2


def feed_forward(nc, tag, x_in, x_out, weights, bp, b2, gamma, beta):
    n = x_in.shape[0] // GROUP

    with ExitStack() as es:
        def sb(name, shape, dt):
            return es.enter_context(nc.sbuf_tensor(tag + name, shape, dt))

        def bank(name, banks=1):
            return es.enter_context(nc.psum_tensor(tag + name, [P, banks * 512], F32))

        def sem(name):
            return es.enter_context(nc.semaphore(tag + name))

        wp_hi = sb("wp_hi", [P, KT, 2 * FF], F32R)
        wp_lo = sb("wp_lo", [P, KT, 2 * FF], F32R)
        w2_hi = sb("w2_hi", [P, HT, DIM], F32R)
        w2_lo = sb("w2_lo", [P, HT, DIM], F32R)
        bp_c = sb("bp", [P, 2 * HT], F32)
        b2_row = sb("b2", [P, DIM], F32)
        gamma_c = sb("gamma", [P, KT], F32)
        beta_c = sb("beta", [P, KT], F32)
        ident = sb("ident", [P, P], F32)
        pause = sb("pause", [P, 1], F32)
        minus_half = sb("minus_half", [P, GT], F32)
        xt = sb("xt", [P, 2, GT, DIM], F32)
        xres = sb("xres", [P, GT, DIM], F32)
        xnorm = sb("xnorm", [P, GT, DIM], F32)
        yout = sb("yout", [P, GT, DIM], F32)
        stats = sb("stats", [P, GT, 6], F32)
        meanvar = sb("meanvar", [P, GT, 2], F32)
        var_eps = sb("var_eps", [P, GT], F32)
        rstd = sb("rstd", [P, GT], F32)
        h_t = sb("h_t", [P, KT, GTOK], F32)
        h_hi = sb("h_hi", [P, 2, KT, GTOK], F32R)
        h_lo = sb("h_lo", [P, 2, KT, GTOK], F32R)
        gelu = sb("gelu", [P, 2, GTOK], F32)
        gated = sb("gated", [P, 2, GTOK], F32)
        u_hi = sb("u_hi", [P, 2, GTOK], F32R)
        u_lo = sb("u_lo", [P, 2, GTOK], F32R)

        ps_gate = [bank("ps_gate0"), bank("ps_gate1")]
        ps_a = [bank("ps_a0"), bank("ps_a1")]
        ps_y = bank("ps_y", 2)
        ps_ht = bank("ps_ht", 2)

        consts_loaded = sem("consts_loaded")
        w_hi_ready = sem("w_hi_ready")
        w_ready = sem("w_ready")
        ident_made = sem("ident_made")
        half_made = sem("half_made")
        x_loaded = [sem("x_loaded0"), sem("x_loaded1")]
        y_stored = sem("y_stored")
        xres_ready = sem("xres_ready")
        stats_ready = sem("stats_ready")
        meanvar_ready = sem("meanvar_ready")
        var_ready = sem("var_ready")
        rstd_ready = sem("rstd_ready")
        xnorm_ready = sem("xnorm_ready")
        h_transposed = sem("h_transposed")
        h_t_ready = sem("h_t_ready")
        h_hi_ready = sem("h_hi_ready")
        h_ready = sem("h_ready")
        gate_done = sem("gate_done")
        a_done = sem("a_done")
        gelu_ready = sem("gelu_ready")
        gated_ready = sem("gated_ready")
        u_hi_ready = sem("u_hi_ready")
        u_ready = sem("u_ready")
        down_done = sem("down_done")
        y_added = sem("y_added")

        x_in = x_in.rearrange("(n s) q d -> n (s q) d", s=GROUP)
        x_out = x_out.rearrange("(n s) q d -> n (s q) d", s=GROUP)

        def rows(group):
            return group.rearrange("(t p) d -> p t d", p=P)

        def groups(eng, step):
            for j in range(HT):
                step(0, 0, j, FIRST)
            with eng.Fori(1, n - 1, 2) as b:
                for j in range(HT):
                    step(b, 1, j, LOOP)
                for j in range(HT):
                    step(b + 1, 0, j, LOOP)
            for j in range(HT):
                step(n - 1, 1, j, LAST)
            for j in range(DOWN):
                step(n, 0, j, DRAIN)

        block = es.enter_context(nc.Block())

        @block.sync
        def _(sp):
            def load(b, parity):
                if counts(c := b - 1):
                    sp.wait_ge(xnorm_ready, c)
                    sp.wait_ge(xres_ready, c)
                sp.dma_start(xt[:, parity], rows(x_in[b])).then_inc(x_loaded[parity], 16)

            def store(b):
                sp.wait_ge(y_added, 2 * (b + 1))
                sp.dma_start(rows(x_out[b]), yout[:]).then_inc(y_stored, 16)

            load(0, 0)
            load(1, 1)
            load(2, 0)
            with sp.Fori(1, n - 3, 2) as b:
                store(b - 1)
                load(b + 2, 1)
                store(b)
                load(b + 3, 0)
            store(n - 4)
            load(n - 1, 1)
            for b in range(n - 3, n):
                store(b)
            sp.wait_ge(y_stored, 16 * n)

        @block.gpsimd
        def _(pool):
            make_identity(nc, pool, ident, ident_made)
            pool.memset(minus_half[:], -0.5).then_inc(half_made, 1)
            pool.wait_ge(half_made, 1)

            def norm_power(b):
                pool.wait_ge(var_ready, b + 1)
                if counts(c := b):
                    pool.wait_ge(xnorm_ready, c)
                pool.tensor_tensor(rstd[:], var_eps[:], minus_half[:], ALU.pow).then_inc(rstd_ready, 1)

            def residual(b, parity):
                pool.wait_ge(x_loaded[parity], 8 * (b - parity) + 16)
                if counts(c := 2 * b):
                    pool.wait_ge(y_added, c)
                if counts(c := 16 * b):
                    pool.wait_ge(y_stored, c)
                bias = b2_row[:].unsqueeze(1).to_broadcast([P, GT, DIM])
                pool.tensor_tensor(xres[:], xt[:, parity], bias, ALU.add).then_inc(xres_ready, 1)

            norm_power(0)
            pool.wait_ge(consts_loaded, 64)
            residual(0, 0)
            norm_power(1)
            with pool.Fori(1, n - 1, 2) as b:
                for parity in (1, 0):
                    residual(b + 1 - parity, parity)
                    norm_power(b + 2 - parity)
            residual(n - 1, 1)

        @block.scalar
        def _(act):
            with nc.allow_non_contiguous_dma(reason="columns of 128 scales"):
                act.dma_start(gamma_c[:], gamma.rearrange("(k p) -> p k", p=P)).then_inc(consts_loaded, 16)
                act.dma_start(beta_c[:], beta.rearrange("(k p) -> p k", p=P)).then_inc(consts_loaded, 16)
                act.dma_start(bp_c[:], bp.rearrange("(k p) -> p k", p=P)).then_inc(consts_loaded, 16)
            act.dma_start(b2_row[:], b2.partition_broadcast(P)).then_inc(consts_loaded, 16)
            act.wait_ge(weights.loaded["wp"], 16)
            for cols in WP_PARTS:
                act.activation(wp_hi[:, :, cols], weights.raw_wp[:, :, cols], ACT.Copy).then_inc(w_hi_ready, 1)
            act.wait_ge(weights.loaded["w2"], 16)
            act.activation(w2_hi[:], weights.raw_w2, ACT.Copy).then_inc(w_hi_ready, 1)
            act.wait_ge(consts_loaded, 64)

            def step(b, parity, j, part):
                if part == DRAIN:
                    return
                i = HT * b + j
                slot = j % 2
                act.wait_ge(gate_done, i + 1)
                if counts(c := i - 1):
                    act.wait_ge(gated_ready, c)
                act.activation(gelu[:, slot], ps_gate[slot][:], ACT.Gelu,
                               bias=bp_c[:, HT + j:HT + j + 1]).then_inc(gelu_ready, 1)
                act.wait_ge(gated_ready, i + 1)
                if counts(c := i - 1):
                    act.wait_ge(down_done, c)
                act.activation(u_hi[:, slot], gated[:, slot], ACT.Copy).then_inc(u_hi_ready, 1)

            groups(act, step)

        @block.vector
        def _(dve):
            def norm_stats(b, parity):
                dve.wait_ge(x_loaded[parity], 8 * (b - parity) + 16)
                for t in range(GT):
                    nc.vector.bn_stats(stats[:, t], xt[:, parity, t]).then_inc(stats_ready, 1)
                dve.wait_ge(stats_ready, GT * (b + 1))
                nc.vector.memset(pause[:], 0.0)
                for t in range(GT):
                    nc.vector.bn_aggr(meanvar[:, t], stats[:, t]).then_inc(meanvar_ready, 1)
                dve.wait_ge(meanvar_ready, GT * (b + 1))
                nc.vector.tensor_scalar(var_eps[:], meanvar[:, :, 1], EPS, None, ALU.add).then_inc(var_ready, 1)

            def norm_apply(b, parity):
                dve.wait_ge(rstd_ready, b + 1)
                if counts(c := b):
                    dve.wait_ge(h_transposed, c)
                for t in range(GT):
                    last = nc.vector.tensor_scalar(xnorm[:, t], xt[:, parity, t], meanvar[:, t, 0:1], rstd[:, t:t + 1],
                                                   ALU.subtract, ALU.mult)
                last.then_inc(xnorm_ready, 1)

            def scale_shift(b):
                dve.wait_ge(h_transposed, b + 1)
                for k in range(KT):
                    last = nc.vector.tensor_scalar(h_t[:, k], ps_ht[:, k * GTOK:(k + 1) * GTOK], gamma_c[:, k:k + 1],
                                                   beta_c[:, k:k + 1], ALU.mult, ALU.add)
                last.then_inc(h_t_ready, 1)

            def split_h(b, parity):
                dve.wait_ge(h_t_ready, b + 1)
                if counts(c := HT * (b - 1)):
                    dve.wait_ge(a_done, c)
                nc.vector.tensor_copy(h_hi[:, parity], h_t[:]).then_inc(h_hi_ready, 1)
                dve.wait_ge(h_hi_ready, b + 1)
                nc.vector.tensor_tensor(h_lo[:, parity], h_t[:], h_hi[:, parity].bitcast(F32),
                                        ALU.subtract).then_inc(h_ready, 1)

            norm_stats(0, 0)
            norm_apply(0, 0)
            dve.wait_ge(consts_loaded, 64)
            scale_shift(0)
            split_h(0, 0)
            for i, cols in enumerate(WP_PARTS):
                dve.wait_ge(w_hi_ready, i + 1)
                nc.vector.tensor_tensor(wp_lo[:, :, cols], weights.raw_wp[:, :, cols], wp_hi[:, :, cols].bitcast(F32),
                                        ALU.subtract).then_inc(w_ready, 1)
            dve.wait_ge(w_hi_ready, len(WP_PARTS) + 1)
            nc.vector.tensor_tensor(w2_lo[:], weights.raw_w2, w2_hi[:].bitcast(F32), ALU.subtract).then_inc(w_ready, 1)

            def step(b, parity, j, part):
                i = HT * b + j
                slot = j % 2
                if part != DRAIN:
                    dve.wait_ge(a_done, i + 1)
                    dve.wait_ge(gelu_ready, i + 1)
                    if counts(c := i - 1):
                        dve.wait_ge(u_ready, c)
                    nc.vector.scalar_tensor_tensor(gated[:, slot], ps_a[slot][:], bp_c[:, j:j + 1], gelu[:, slot],
                                                   ALU.add, ALU.mult).then_inc(gated_ready, 1)
                if j == DOWN - 1 and part != FIRST:
                    dve.wait_ge(down_done, HT * b)
                    dve.wait_ge(xres_ready, b)
                    for half in range(2):
                        r = slice(half * TT, (half + 1) * TT)
                        nc.vector.tensor_tensor(yout[:, r].rearrange("p t d -> p (t d)"),
                                                ps_y[:, half * 512:(half + 1) * 512],
                                                xres[:, r].rearrange("p t d -> p (t d)"),
                                                ALU.add).then_inc(y_added, 1)
                if part != DRAIN:
                    dve.wait_ge(u_hi_ready, i + 1)
                    if counts(c := i - 1):
                        dve.wait_ge(down_done, c)
                    nc.vector.tensor_tensor(u_lo[:, slot], gated[:, slot], u_hi[:, slot].bitcast(F32),
                                            ALU.subtract).then_inc(u_ready, 1)
                if part in (FIRST, LOOP):
                    if j == 2:
                        norm_stats(b + 1, 1 - parity)
                    if j == 3:
                        norm_apply(b + 1, 1 - parity)
                    if j == 5:
                        scale_shift(b + 1)
                    if j == 6:
                        split_h(b + 1, 1 - parity)

            groups(dve, step)

        @block.tensor
        def _(pe):
            def transpose_h(b):
                pe.wait_ge(xnorm_ready, b + 1)
                if counts(c := b):
                    pe.wait_ge(h_t_ready, c)
                for k in range(KT):
                    for t in range(GT):
                        last = nc.tensor.transpose(ps_ht[:, k * GTOK + t * P:k * GTOK + (t + 1) * P],
                                                   xnorm[:, t, k * P:(k + 1) * P], ident[:])
                last.then_inc(h_transposed, 1)

            def up(out, column, parity, done):
                passes = [t for k in range(KT) for t in ((wp_hi, h_hi, k), (wp_hi, h_lo, k), (wp_lo, h_hi, k))]
                for i, (w, h, k) in enumerate(passes):
                    last = nc.tensor.matmul(out, w[:, k, column:column + P], h[:, parity, k], start=i == 0, stop=i == 5)
                last.then_inc(done, 1)

            def step(b, parity, j, part):
                i = HT * b + j
                slot = j % 2
                if part != DRAIN:
                    pe.wait_ge(h_ready, b + 1)
                    if part == FIRST and j % 4 == 0:
                        pe.wait_ge(w_ready, 2 * (j // 4 + 1))
                    if counts(c := i - 1):
                        pe.wait_ge(gelu_ready, c)
                    up(ps_gate[slot][:], FF + j * P, parity, gate_done)
                    if counts(c := i - 1):
                        pe.wait_ge(gated_ready, c)
                    up(ps_a[slot][:], j * P, parity, a_done)
                if alive(part, j, DOWN):
                    q = (j - DOWN) % HT
                    pe.wait_ge(u_ready, i - DOWN + 1)
                    if part == FIRST and q == 0:
                        pe.wait_ge(w_ready, len(WP_PARTS) + 1)
                    if q == 0:
                        if counts(c := 2 * b):
                            pe.wait_ge(y_added, c)
                    for t in range(GT):
                        for s, (a, m) in enumerate(((u_hi, w2_hi), (u_lo, w2_hi), (u_hi, w2_lo))):
                            last = nc.tensor.matmul(ps_y[:, t * DIM:(t + 1) * DIM], a[:, q % 2, t * P:(t + 1) * P],
                                                    m[:, q], start=q == 0 and t % 2 == 0 and s == 0,
                                                    stop=q == HT - 1 and t % 2 == 1 and s == 2,
                                                    skip_group_check=True)
                    last.then_inc(down_done, 1)
                if part in (FIRST, LOOP) and j == 4:
                    transpose_h(b + 1)

            pe.wait_ge(ident_made, 2)
            transpose_h(0)
            groups(pe, step)


_W = "L0_xattn_"
_INS = ["x", "ctx_768"] + [_W + w for w in (
    "Wq1", "Wk1", "Wv1", "Wo1", "bo1", "Wq2", "Wk2", "Wv2", "Wo2", "bo2", "Wp", "bp", "W2", "b2",
    "g1", "be1", "g2", "be2", "g3", "be3")]


def block_program(nc, a, out):
    x1 = nc.dram_tensor("after_self_attention", a["x"].shape, F32).ap()
    x2 = nc.dram_tensor("after_cross_attention", a["x"].shape, F32).ap()
    w = {k[len(_W):]: v for k, v in a.items() if k.startswith(_W)}
    with ExitStack() as es:
        raw = [es.enter_context(nc.sbuf_tensor(f"raw{i}", [P, len(WEIGHTS) * W_COLS], F32)) for i in range(2)]

        def loaded(tag, names):
            return {k: es.enter_context(nc.semaphore(f"{tag}loaded_{k}")) for k in names}

        self_w = AttentionWeights(raw[0], loaded("self_", WEIGHTS), [w[k] for k in ("Wq1", "Wk1", "Wv1", "Wo1")], False)
        cross_w = AttentionWeights(raw[1], loaded("cross_", WEIGHTS), [w[k] for k in ("Wq2", "Wk2", "Wv2", "Wo2")], True)
        ff_w = FeedForwardWeights(raw[0], loaded("ff_", ("wp", "w2")), w["Wp"], w["W2"])
        attention(nc, "self_", a["x"], None, x1, self_w, w["bo1"], w["g1"], w["be1"], cross_w.load)
        attention(nc, "cross_", x1, a["ctx_768"], x2, cross_w, w["bo2"], w["g2"], w["be2"], ff_w.load)
        feed_forward(nc, "ff_", x2, out, ff_w, w["bp"], w["b2"], w["g3"], w["be3"])


def kernel(**inputs):
    import numpy as np
    import concourse.bacc as bacc
    from concourse.bass_utils import run_bass_kernel_spmd

    nc = bacc.Bacc("TRN2", target_bir_lowering=False, num_devices=1)
    arrays, aps = {}, {}
    for name in _INS:
        arrays["in_" + name] = np.ascontiguousarray(inputs[name])
        aps[name] = nc.dram_tensor("in_" + name, arrays["in_" + name].shape, F32, kind="ExternalInput").ap()
    out = nc.dram_tensor("out", arrays["in_x"].shape, F32, kind="ExternalOutput").ap()
    block_program(nc, aps, out)
    r = run_bass_kernel_spmd(nc, [arrays], core_ids=[0])
    return r.results[0]["out"]
```

```python
from contextlib import ExitStack

import concourse.bass as bass
from concourse import mybir

F32 = mybir.dt.float32
F32R = mybir.dt.float32r
ALU = mybir.AluOpType
ACT = mybir.ActivationFunctionType
AX_X = mybir.AxisListType.X

P = 128
DIM = 256
KT = DIM // P
SEQ = 256
TT = SEQ // P
HEADS = 16
DHEAD = 64
INNER = HEADS * DHEAD
PAIRS = HEADS // 2
CTX = 192
FF = 4 * DIM
EPS = 1e-5
SCALE = DHEAD ** -0.5

OWN = (slice(0, DHEAD), slice(DHEAD, P))
OTHER = OWN[::-1]
RING = 4
SCORES, TRANSPOSED, WEIGHTED, PROJECTED = 1, 3, 4, 5
V_PARTS = ((0, (0,)), (0, (1,)), (1, (0,)), (1, (1,)), (2, (0, 1)), (3, (0,)), (3, (1,)))
V_READY = (2, 4, 5, 7)
V_COLS = INNER // 4
FIRST, LOOP, LAST, DRAIN = range(4)


def counts(c):
    return not isinstance(c, int) or c > 0


def sequences(nc, eng, n, step):
    for p in range(PAIRS):
        step(0, p, FIRST)
    with nc.Fori(1, n - 1, engines=[eng.engine], hint_back_edge=True) as b:
        for p in range(PAIRS):
            step(b, p, LOOP)
    for p in range(PAIRS):
        step(n - 1, p, LAST)
    for p in range(PROJECTED):
        step(n, p, DRAIN)


def alive(part, p, lag):
    return p >= lag if part == FIRST else p < lag if part == DRAIN else True


def make_identity(nc, pool, ident, made):
    pool.memset(ident[:], 0.0).then_inc(made, 1)
    pool.wait_ge(made, 1)
    pool.affine_select(out=ident[:], in_=ident[:], compare_op=ALU.not_equal, fill=1.0, base=0,
                       pattern=[[-1, P]], channel_multiplier=1).then_inc(made, 1)


WEIGHTS = ("wq", "wk", "wv", "wo")
W_COLS = KT * INNER


class AttentionWeights:

    def __init__(self, buffer, loaded, sources, prefetched):
        self.buffer, self.loaded, self.prefetched = buffer, loaded, prefetched
        self.sources = dict(zip(WEIGHTS, sources))

    def raw(self, w):
        i = WEIGHTS.index(w)
        return self.buffer[:, i * W_COLS:(i + 1) * W_COLS]

    def count(self, w):
        return 48 if self.sources[w].shape[0] == CTX else 16

    def load(self, sp):
        for w, src in self.sources.items():
            dst = self.raw(w)
            if src.shape[0] == CTX:
                sp.dma_start(dst[:, 0:INNER], src[0:P, :]).then_inc(self.loaded[w], 16)
                sp.dma_start(dst[0:CTX - P, INNER:], src[P:CTX, :]).then_inc(self.loaded[w], 16)
                sp.dma_start(dst[CTX - P:P, INNER:], src[P:CTX, :]).then_inc(self.loaded[w], 16)
            else:
                sp.dma_start(dst.rearrange("p (k n) -> p k n", n=src.shape[1]),
                             src.rearrange("(k p) n -> p k n", p=P)).then_inc(self.loaded[w], 16)


class FeedForwardWeights:

    def __init__(self, buffer, loaded, wp, w2):
        self.loaded, self.wp, self.w2 = loaded, wp, w2
        self.raw_wp = buffer[:, 0:2 * W_COLS].rearrange("p (k n) -> p k n", k=KT)
        self.raw_w2 = buffer[:, 2 * W_COLS:3 * W_COLS].rearrange("p (k n) -> p k n", n=DIM)

    def load(self, sp):
        sp.dma_start(self.raw_wp, self.wp.rearrange("(k p) n -> p k n", p=P)).then_inc(self.loaded["wp"], 16)
        sp.dma_start(self.raw_w2, self.w2.rearrange("(k p) n -> p k n", p=P)).then_inc(self.loaded["w2"], 16)


def attention(nc, tag, x_in, ctx_in, x_out, weights, bo, gamma, beta, prefetch, yout, y_stored, before):
    n = x_in.shape[0]
    cross = ctx_in is not None

    with ExitStack() as es:
        def sb(name, shape, dt):
            return es.enter_context(nc.sbuf_tensor(tag + name, shape, dt))

        def bank(name, banks=1):
            return es.enter_context(nc.psum_tensor(tag + name, [P, banks * 512], F32))

        def sem(name):
            return es.enter_context(nc.semaphore(tag + name))

        w_hi = {w: sb("hi_" + w, [P, W_COLS], F32R) for w in WEIGHTS}
        w_lo = {w: sb("lo_" + w, [P, W_COLS], F32R) for w in WEIGHTS}
        by_k = {w: (w_hi[w][:].rearrange("p (k n) -> p k n", k=KT), w_lo[w][:].rearrange("p (k n) -> p k n", k=KT))
                for w in ("wq", "wk", "wv")}
        wo_hi = w_hi["wo"][:].rearrange("p (k n) -> p k n", k=PAIRS)
        wo_lo = w_lo["wo"][:].rearrange("p (k n) -> p k n", k=PAIRS)
        gamma_c = sb("gamma", [P, KT], F32)
        beta_c = sb("beta", [P, KT], F32)
        bo_row = sb("bo", [P, DIM], F32)
        ident = sb("ident", [P, P], F32)
        pause = sb("pause", [P, 1], F32)
        minus_half = sb("minus_half", [P, TT], F32)

        xt = sb("xt", [P, TT, DIM], F32)
        xres = sb("xres", [P, TT, DIM], F32)
        xnorm = sb("xnorm", [P, TT, DIM], F32)
        stats = sb("stats", [P, TT, 6], F32)
        meanvar = sb("meanvar", [P, TT, 2], F32)
        var_eps = sb("var_eps", [P, TT], F32)
        rstd = sb("rstd", [P, TT], F32)
        h_t = sb("h_t", [P, KT, SEQ], F32)
        h_hi = sb("h_hi", [P, KT, SEQ], F32R)
        h_lo = sb("h_lo", [P, KT, SEQ], F32R)
        if cross:
            ct = sb("ct", [P, TT, DIM], F32)
            c_t = sb("c_t", [P, KT, SEQ], F32)
            c_hi = sb("c_hi", [P, KT, SEQ], F32R)
            c_lo = sb("c_lo", [P, SEQ], F32R)
        q_cat = sb("q_cat", [P, 2, 2, SEQ], F32R)
        k_cat = sb("k_cat", [P, 2, 2, SEQ], F32R)
        k_hi = sb("k_hi", [P, 2, SEQ], F32R)
        v = sb("v", [P, TT, INNER], F32)
        probs = sb("probs", [P, RING, 2, TT, SEQ], F32)
        probs_t = sb("probs_t", [P, 2, 2, TT, SEQ], F32)
        row_max = sb("row_max", [P, 2 * TT], F32)
        neg_max = sb("neg_max", [P, 2 * TT], F32)
        row_sum = sb("row_sum", [P, RING, 2 * TT], F32)
        row_inv = sb("row_inv", [P, RING, 2 * TT], F32)
        o_hi = sb("o_hi", [P, 2, SEQ], F32R)
        o_lo = sb("o_lo", [P, 2, SEQ], F32R)

        ps_qk = bank("ps_qk")
        ps_s = bank("ps_s", 2)
        ps_pt = [bank("ps_pt0"), bank("ps_pt1")]
        ps_o = bank("ps_o")
        ps_y = bank("ps_y")
        ps_misc = bank("ps_misc")
        scores = ps_s[:].rearrange("p (h t k) -> p h t k", h=2, t=TT)

        consts_loaded = sem("consts_loaded")
        w_hi_ready = sem("w_hi_ready")
        w_ready = sem("w_ready")
        wo_ready = sem("wo_ready")
        ident_made = sem("ident_made")
        half_made = sem("half_made")
        x_loaded = sem("x_loaded")
        residual_loaded = sem("residual_loaded")
        ctx_loaded = sem("ctx_loaded")
        xres_ready = sem("xres_ready")
        stats_ready = sem("stats_ready")
        meanvar_ready = sem("meanvar_ready")
        var_ready = sem("var_ready")
        rstd_ready = sem("rstd_ready")
        xnorm_ready = sem("xnorm_ready")
        h_transposed = sem("h_transposed")
        h_t_ready = sem("h_t_ready")
        h_hi_ready = sem("h_hi_ready")
        h_ready = sem("h_ready")
        c_transposed = sem("c_transposed")
        c_t_ready = sem("c_t_ready")
        c_hi_ready = sem("c_hi_ready")
        c_ready = sem("c_ready")
        qk_done = sem("qk_done")
        qk_hi_ready = sem("qk_hi_ready")
        qk_lo_ready = sem("qk_lo_ready")
        qk_ready = sem("qk_ready")
        v_done = sem("v_done")
        v_ready = sem("v_ready")
        scores_done = sem("scores_done")
        max_ready = sem("max_ready")
        neg_max_ready = sem("neg_max_ready")
        exps_done = sem("exps_done")
        inv_ready = sem("inv_ready")
        probs_ready = sem("probs_ready")
        probs_transposed = sem("probs_transposed")
        probs_t_ready = sem("probs_t_ready")
        pv_done = sem("pv_done")
        o_hi_ready = sem("o_hi_ready")
        o_ready = sem("o_ready")
        wo_done = sem("wo_done")
        y_added = sem("y_added")

        def rows(seq):
            return seq.rearrange("(t p) d -> p t d", p=P)

        block = es.enter_context(nc.Block())

        @block.sync
        def _(sp):
            def load_context(b):
                c = rows(ctx_in[b])
                sp.dma_start(ct[:, :, 0:CTX], c).then_inc(ctx_loaded, 16)
                sp.dma_start(ct[:, :, CTX:DIM], c[:, :, P:CTX]).then_inc(ctx_loaded, 16)

            sp.dma_start(xt[:], rows(x_in[0])).then_inc(x_loaded, 16)
            if cross:
                load_context(0)
            if not weights.prefetched:
                weights.load(sp)

            def load_next(b):
                sp.wait_ge(xnorm_ready, b)
                sp.dma_start(xt[:], rows(x_in[b])).then_inc(x_loaded, 16)
                if cross:
                    sp.wait_ge(c_transposed, b)
                    load_context(b)

            def load_residual(b):
                if counts(c := b):
                    sp.wait_ge(y_added, c)
                sp.dma_start(xres[:], rows(x_in[b])).then_inc(residual_loaded, 16)

            def store(b):
                sp.wait_ge(y_added, b + 1)
                sp.dma_start(rows(x_out[b]), yout[:]).then_inc(y_stored, 16)

            load_residual(0)
            if before is not None:
                sp.wait_ge(before, 16 * n)
            load_next(1)
            prefetch(sp)
            with sp.Fori(1, n - 1) as b:
                load_next(b + 1)
                store(b - 1)
                load_residual(b)
            store(n - 2)
            load_residual(n - 1)
            store(n - 1)

        @block.gpsimd
        def _(pool):
            make_identity(nc, pool, ident, ident_made)
            pool.memset(minus_half[:], -0.5).then_inc(half_made, 1)
            pool.wait_ge(half_made, 1)

            def norm_power(b):
                pool.wait_ge(var_ready, b + 1)
                if counts(c := b):
                    pool.wait_ge(xnorm_ready, c)
                pool.tensor_tensor(rstd[:], var_eps[:], minus_half[:], ALU.pow).then_inc(rstd_ready, 1)

            def low_h(b):
                pool.wait_ge(h_hi_ready, b + 1)
                pool.tensor_tensor(h_lo[:], h_t[:], h_hi[:].bitcast(F32), ALU.subtract).then_inc(h_ready, 1)

            def low_context(b):
                pool.wait_ge(c_hi_ready, b + 1)
                pool.wait_ge(h_ready, b + 1)
                pool.tensor_tensor(c_lo[:], c_t[:, 0], c_hi[:, 0].bitcast(F32), ALU.subtract).then_inc(c_ready, 1)

            def residual(b):
                if counts(c := 16 * b):
                    pool.wait_ge(y_stored, c)
                pool.wait_ge(residual_loaded, 16 * (b + 1))
                bias = bo_row[:].unsqueeze(1).to_broadcast([P, TT, DIM])
                pool.tensor_tensor(xres[:], xres[:], bias, ALU.add).then_inc(xres_ready, 1)

            def step(b, p, part):
                g = PAIRS * b + p
                if part in (FIRST, LOOP) and p == 3:
                    norm_power(b + 1)
                if part in (FIRST, LOOP) and p == 7:
                    low_h(b + 1)
                    if cross:
                        low_context(b + 1)
                if part != DRAIN and p == 6:
                    residual(b)
                if alive(part, p, SCORES):
                    s = g - SCORES
                    slot = (p - SCORES) % RING
                    for h in range(2):
                        pool.wait_ge(inv_ready, 2 * s + h + 1)
                        scale = row_inv[:, slot, TT * h:TT * h + TT].unsqueeze(2).to_broadcast([P, TT, SEQ])
                        pool.tensor_tensor(probs[:, slot, h], probs[:, slot, h], scale,
                                           ALU.mult).then_inc(probs_ready, 1)

            norm_power(0)
            low_h(0)
            if cross:
                low_context(0)
            pool.wait_ge(h_ready, 1)
            pool.wait_ge(w_hi_ready, 4)
            pool.tensor_tensor(w_lo["wo"][:], weights.raw("wo"), w_hi["wo"][:].bitcast(F32),
                               ALU.subtract).then_inc(wo_ready, 1)
            pool.wait_ge(consts_loaded, 48)
            sequences(nc, pool, n, step)

        @block.scalar
        def _(act):
            with nc.allow_non_contiguous_dma(reason="columns of 128 scales"):
                act.dma_start(gamma_c[:], gamma.rearrange("(k p) -> p k", p=P)).then_inc(consts_loaded, 16)
                act.dma_start(beta_c[:], beta.rearrange("(k p) -> p k", p=P)).then_inc(consts_loaded, 16)
            act.dma_start(bo_row[:], bo.partition_broadcast(P)).then_inc(consts_loaded, 16)

            def weight_high(w):
                act.wait_ge(weights.loaded[w], weights.count(w))
                act.activation(w_hi[w][:], weights.raw(w), ACT.Copy).then_inc(w_hi_ready, 1)

            def exps(s, slot, h):
                act.wait_ge(neg_max_ready, 2 * s + h + 1)
                if counts(c := 2 * (s - RING + 1)):
                    act.wait_ge(probs_transposed, c)
                for t in range(TT):
                    i = TT * h + t
                    last = act.activation(probs[:, slot, h, t], scores[:, h, t], ACT.Exp, bias=neg_max[:, i:i + 1],
                                          scale=SCALE, accum_out=row_sum[:, slot, i:i + 1])
                last.then_inc(exps_done, 1)

            def scale_shift(b):
                act.wait_ge(h_transposed, b + 1)
                if counts(c := b):
                    act.wait_ge(h_ready, c)
                for k in range(KT):
                    last = act.activation(h_t[:, k], ps_misc[:, k * SEQ:(k + 1) * SEQ], ACT.Identity,
                                          bias=beta_c[:, k:k + 1], scale=gamma_c[:, k:k + 1])
                last.then_inc(h_t_ready, 1)

            def high_h(b):
                act.wait_ge(h_t_ready, b + 1)
                if counts(c := PAIRS * b):
                    act.wait_ge(qk_done, c)
                if counts(c := len(V_PARTS) * b):
                    act.wait_ge(v_done, c)
                act.activation(h_hi[:], h_t[:], ACT.Copy).then_inc(h_hi_ready, 1)

            def high_context(b):
                act.wait_ge(c_t_ready, b + 1)
                if counts(c := PAIRS * b):
                    act.wait_ge(qk_done, c)
                if counts(c := len(V_PARTS) * b):
                    act.wait_ge(v_done, c)
                act.activation(c_hi[:], c_t[:], ACT.Copy).then_inc(c_hi_ready, 1)

            def copy_v(b, p):
                quarter, tiles = V_PARTS[p]
                act.wait_ge(v_done, len(V_PARTS) * b + p + 1)
                if counts(c := PAIRS * (b - 1) + 2 * quarter + 2):
                    act.wait_ge(pv_done, c)
                act.activation(v[:, tiles[0]:tiles[-1] + 1, quarter * V_COLS:(quarter + 1) * V_COLS],
                               ps_misc[:, 0:len(tiles) * V_COLS].rearrange("p (t n) -> p t n", n=V_COLS),
                               ACT.Copy).then_inc(v_ready, 1)

            def step(b, p, part):
                g = PAIRS * b + p
                if part != DRAIN:
                    slot = p % 2
                    act.wait_ge(qk_done, g + 1)
                    if counts(c := 2 * (g - 1)):
                        act.wait_ge(scores_done, c)
                    act.activation(k_hi[:, slot], ps_qk[:, SEQ:2 * SEQ], ACT.Copy)
                    for h in range(2):
                        last = act.activation(q_cat[OWN[h], slot, h], ps_qk[OWN[h], 0:SEQ], ACT.Copy)
                    last.then_inc(qk_hi_ready, 1)
                if part in (FIRST, LOOP) and p == 7:
                    high_h(b + 1)
                    if cross:
                        high_context(b + 1)
                if alive(part, p, SCORES):
                    exps(g - SCORES, (p - SCORES) % RING, 0)
                if part != DRAIN and p < len(V_PARTS):
                    copy_v(b, p)
                if alive(part, p, TRANSPOSED):
                    s = g - TRANSPOSED
                    slot = (p - TRANSPOSED) % 2
                    for h in range(2):
                        act.wait_ge(probs_transposed, 2 * s + h + 1)
                        if counts(c := s - 1):
                            act.wait_ge(pv_done, c)
                        act.activation(probs_t[:, slot, h].rearrange("p t q -> p (t q)"), ps_pt[h][:],
                                       ACT.Copy).then_inc(probs_t_ready, 1)
                if alive(part, p, WEIGHTED):
                    slot = (p - WEIGHTED) % 2
                    act.wait_ge(pv_done, g - WEIGHTED + 1)
                    if counts(c := g - WEIGHTED - 1):
                        act.wait_ge(wo_done, c)
                    act.activation(o_hi[:, slot], ps_o[:, 0:SEQ], ACT.Copy).then_inc(o_hi_ready, 1)
                if alive(part, p, SCORES):
                    exps(g - SCORES, (p - SCORES) % RING, 1)
                if part in (FIRST, LOOP) and p == 6:
                    scale_shift(b + 1)

            weight_high("wq")
            weight_high("wk")
            act.wait_ge(consts_loaded, 48)
            scale_shift(0)
            high_h(0)
            if cross:
                high_context(0)
            weight_high("wv")
            weight_high("wo")
            sequences(nc, act, n, step)

        @block.vector
        def _(dve):
            def norm_stats(b):
                dve.wait_ge(x_loaded, 16 * (b + 1))
                for t in range(TT):
                    nc.vector.bn_stats(stats[:, t], xt[:, t]).then_inc(stats_ready, 1)
                dve.wait_ge(stats_ready, TT * (b + 1))
                nc.vector.memset(pause[:], 0.0)
                for t in range(TT):
                    nc.vector.bn_aggr(meanvar[:, t], stats[:, t]).then_inc(meanvar_ready, 1)
                dve.wait_ge(meanvar_ready, TT * (b + 1))
                nc.vector.tensor_scalar(var_eps[:], meanvar[:, :, 1], EPS, None, ALU.add).then_inc(var_ready, 1)

            def norm_apply(b):
                dve.wait_ge(rstd_ready, b + 1)
                if counts(c := b):
                    dve.wait_ge(h_transposed, c)
                for t in range(TT):
                    last = nc.vector.tensor_scalar(xnorm[:, t], xt[:, t], meanvar[:, t, 0:1], rstd[:, t:t + 1],
                                                   ALU.subtract, ALU.mult)
                last.then_inc(xnorm_ready, 1)

            def context_copy(b):
                dve.wait_ge(c_transposed, b + 1)
                nc.vector.tensor_copy(c_t[:].rearrange("p k q -> p (k q)"), ps_misc[:]).then_inc(c_t_ready, 1)

            def extras(b, p, part):
                if p == PROJECTED - 1 and part != FIRST:
                    dve.wait_ge(wo_done, PAIRS * b)
                    dve.wait_ge(xres_ready, b)
                    nc.vector.tensor_tensor(yout[:].rearrange("p t d -> p (t d)"), ps_y[:],
                                            xres[:].rearrange("p t d -> p (t d)"), ALU.add).then_inc(y_added, 1)
                if part in (FIRST, LOOP):
                    if p == 2:
                        norm_stats(b + 1)
                    if p == 3:
                        norm_apply(b + 1)
                    if p == 5 and cross:
                        context_copy(b + 1)

            def low_context(b):
                dve.wait_ge(c_hi_ready, b + 1)
                nc.vector.tensor_tensor(c_hi[64:P, 1], c_t[64:P, 1], c_hi[64:P, 1].bitcast(F32),
                                        ALU.subtract).then_inc(c_ready, 1)

            def maxima(s, h):
                r = slice(TT * h, TT * h + TT)
                dve.wait_ge(scores_done, 2 * s + h + 1)
                nc.vector.tensor_reduce(row_max[:, r], scores[:, h], AX_X, ALU.max).then_inc(max_ready, 1)
                dve.wait_ge(max_ready, 2 * s + h + 1)
                nc.vector.tensor_scalar(neg_max[:, r], row_max[:, r], -SCALE, None, ALU.mult).then_inc(neg_max_ready, 1)

            def low_parts(g, p):
                slot = p % 2
                dve.wait_ge(qk_hi_ready, g + 1)
                if counts(c := 2 * (g - 1)):
                    dve.wait_ge(scores_done, c)
                for h in range(2):
                    nc.vector.tensor_tensor(k_cat[OWN[h], slot, h], ps_qk[OWN[h], SEQ:2 * SEQ],
                                            k_hi[OWN[h], slot].bitcast(F32), ALU.subtract)
                    last = nc.vector.tensor_tensor(q_cat[OTHER[h], slot, h], ps_qk[OWN[h], 0:SEQ],
                                                   q_cat[OWN[h], slot, h].bitcast(F32), ALU.subtract)
                last.then_inc(qk_lo_ready, 1)

            def other_rows(p):
                slot = p % 2
                for h in range(2):
                    last = nc.vector.tensor_copy(k_cat[OTHER[h], slot, h], k_hi[OWN[h], slot].bitcast(F32))
                last.then_inc(qk_ready, 1)

            def inverse(s, slot, h):
                dve.wait_ge(exps_done, 2 * s + h + 1)
                nc.vector.reciprocal(row_inv[:, slot, TT * h:TT * h + TT],
                                     row_sum[:, slot, TT * h:TT * h + TT]).then_inc(inv_ready, 1)

            def step(b, p, part):
                g = PAIRS * b + p
                s = g - SCORES
                if alive(part, p, PROJECTED):
                    slot = (p - PROJECTED) % 2
                    dve.wait_ge(o_hi_ready, g - PROJECTED + 1)
                    if counts(c := g - PROJECTED - 1):
                        dve.wait_ge(wo_done, c)
                    nc.vector.tensor_tensor(o_lo[:, slot], ps_o[:, 0:SEQ], o_hi[:, slot].bitcast(F32),
                                            ALU.subtract).then_inc(o_ready, 1)
                if alive(part, p, SCORES):
                    maxima(s, 0)
                if part != DRAIN:
                    low_parts(g, p)
                if alive(part, p, SCORES):
                    maxima(s, 1)
                if part in (FIRST, LOOP) and p == 7 and cross:
                    low_context(b + 1)
                if alive(part, p, SCORES):
                    inverse(s, (p - SCORES) % RING, 0)
                if part != DRAIN:
                    other_rows(p)
                if alive(part, p, SCORES):
                    inverse(s, (p - SCORES) % RING, 1)
                extras(b, p, part)

            norm_stats(0)
            norm_apply(0)
            if cross:
                context_copy(0)
            for i, w in enumerate(("wq", "wk", "wv")):
                if w == "wv" and cross:
                    low_context(0)
                dve.wait_ge(w_hi_ready, i + 1)
                nc.vector.tensor_tensor(w_lo[w][:], weights.raw(w), w_hi[w][:].bitcast(F32),
                                        ALU.subtract).then_inc(w_ready, 1)
            sequences(nc, dve, n, step)

        @block.tensor
        def _(pe):
            def terms(source_h, w):
                hi, lo = by_k[w]
                if source_h:
                    for k in range(KT):
                        yield h_hi[:, k], hi[:, k]
                        yield h_lo[:, k], hi[:, k]
                        yield h_hi[:, k], lo[:, k]
                else:
                    yield c_hi[:, 0], hi[:, 0]
                    yield c_lo[:], hi[:, 0]
                    yield c_hi[:, 0], lo[:, 0]
                    yield c_hi[:, 1], hi[:, 1]
                    yield c_hi[:, 1], lo[:, 1]

            def project_pair(out, p, source_h, w):
                passes = list(terms(source_h, w))
                for i, (a, m) in enumerate(passes):
                    last = nc.tensor.matmul(out, m[:, p * P:(p + 1) * P], a, start=i == 0, stop=i == len(passes) - 1)
                return last

            def project_v(b, p, part):
                quarter, tiles = V_PARTS[p]
                if counts(c := len(V_PARTS) * b + p):
                    pe.wait_ge(v_ready, c)
                if cross and part in (FIRST, LOOP) and p == 6:
                    pe.wait_ge(c_t_ready, b + 2)
                if part == FIRST and p == 0:
                    pe.wait_ge(w_ready, 3)
                passes = list(terms(not cross, "wv"))
                for i, t in enumerate(tiles):
                    for j, (a, m) in enumerate(passes):
                        last = nc.tensor.matmul(ps_misc[:, i * V_COLS:(i + 1) * V_COLS], a[:, t * P:(t + 1) * P],
                                                m[:, quarter * V_COLS:(quarter + 1) * V_COLS],
                                                start=j == 0, stop=j == len(passes) - 1)
                last.then_inc(v_done, 1)

            def transposes(src, done):
                for k in range(KT):
                    for t in range(TT):
                        last = nc.tensor.transpose(ps_misc[:, k * SEQ + t * P:k * SEQ + (t + 1) * P],
                                                   src[:, t, k * P:(k + 1) * P], ident[:])
                last.then_inc(done, 1)

            def transpose_h(b):
                pe.wait_ge(xnorm_ready, b + 1)
                if counts(c := len(V_PARTS) * b):
                    pe.wait_ge(v_ready, c)
                if cross:
                    pe.wait_ge(c_t_ready, b + 1)
                transposes(xnorm, h_transposed)

            def transpose_context(b):
                pe.wait_ge(ctx_loaded, 32 * (b + 1))
                if counts(c := len(V_PARTS) * b - 1):
                    pe.wait_ge(v_ready, c)
                transposes(ct, c_transposed)

            def step(b, p, part):
                g = PAIRS * b + p
                if part != DRAIN:
                    pe.wait_ge(h_ready, b + 1)
                    if counts(c := g):
                        pe.wait_ge(qk_lo_ready, c)
                    project_pair(ps_qk[:, 0:SEQ], p, True, "wq")
                    if cross:
                        pe.wait_ge(c_ready, 2 * (b + 1))
                    project_pair(ps_qk[:, SEQ:2 * SEQ], p, not cross, "wk").then_inc(qk_done, 1)
                if alive(part, p, SCORES):
                    s = g - SCORES
                    slot = (p - SCORES) % 2
                    pe.wait_ge(qk_ready, s + 1)
                    for h in range(2):
                        if counts(c := 2 * (s - 1) + h + 1):
                            pe.wait_ge(exps_done, c)
                        for t in range(TT):
                            nc.tensor.matmul(scores[:, h, t], q_cat[OWN[h], slot, h, t * P:(t + 1) * P],
                                             k_hi[OWN[h], slot], start=t == 0, stop=False, skip_group_check=True)
                        for t in range(TT):
                            last = nc.tensor.matmul(scores[:, h, t], q_cat[:, slot, h, t * P:(t + 1) * P],
                                                    k_cat[:, slot, h], start=False, stop=t == TT - 1,
                                                    skip_group_check=True)
                        last.then_inc(scores_done, 1)
                if part != DRAIN and p < len(V_PARTS):
                    project_v(b, p, part)
                if alive(part, p, TRANSPOSED):
                    s = g - TRANSPOSED
                    slot = (p - TRANSPOSED) % RING
                    for h in range(2):
                        pe.wait_ge(probs_ready, 2 * s + h + 1)
                        if counts(c := 2 * (s - 1) + h + 1):
                            pe.wait_ge(probs_t_ready, c)
                        for k in range(TT):
                            for t in range(TT):
                                last = nc.tensor.transpose(ps_pt[h][:, k * SEQ + t * P:k * SEQ + (t + 1) * P],
                                                           probs[:, slot, h, t, k * P:(k + 1) * P], ident[:])
                        last.then_inc(probs_transposed, 1)
                if alive(part, p, WEIGHTED):
                    s = g - WEIGHTED
                    q = (p - WEIGHTED) % PAIRS
                    seq = b if p >= WEIGHTED else b - 1
                    pe.wait_ge(v_ready, len(V_PARTS) * seq + V_READY[q // 2])
                    if counts(c := s):
                        pe.wait_ge(o_ready, c)
                    if counts(c := 2 * s + 2):
                        pe.wait_ge(probs_t_ready, c)
                    for k in range(TT):
                        for h in range(2):
                            c = (2 * q + h) * DHEAD
                            last = nc.tensor.matmul(
                                ps_o[DHEAD * h:DHEAD * (h + 1), 0:SEQ],
                                v[:, k, c:c + DHEAD], probs_t[:, q % 2, h, k], start=k == 0, stop=k == TT - 1)
                    last.then_inc(pv_done, 1)
                if alive(part, p, PROJECTED):
                    s = g - PROJECTED
                    q = (p - PROJECTED) % PAIRS
                    pe.wait_ge(o_ready, s + 1)
                    if part == FIRST and q == 0:
                        pe.wait_ge(wo_ready, 1)
                    if q == 0:
                        if counts(c := b):
                            pe.wait_ge(y_added, c)
                    for t in range(TT):
                        for i, (a, m) in enumerate(((o_hi, wo_hi), (o_lo, wo_hi), (o_hi, wo_lo))):
                            last = nc.tensor.matmul(ps_y[:, t * DIM:(t + 1) * DIM], a[:, q % 2, t * P:(t + 1) * P],
                                                    m[:, q], start=q == 0 and t == 0 and i == 0,
                                                    stop=q == PAIRS - 1 and t == TT - 1 and i == 2,
                                                    skip_group_check=True)
                    last.then_inc(wo_done, 1)
                if part in (FIRST, LOOP):
                    if p == 5 and cross:
                        transpose_context(b + 1)
                    if p == 6:
                        transpose_h(b + 1)

            pe.wait_ge(ident_made, 2)
            if cross:
                transpose_context(0)
            transpose_h(0)
            pe.wait_ge(w_ready, 2)
            sequences(nc, pe, n, step)


GROUP = 2
GT = GROUP * TT
GTOK = GROUP * SEQ
HT = FF // P
WP_PARTS = (slice(FF, FF + 512), slice(0, 512), slice(FF + 512, 2 * FF), slice(512, FF))
DOWN = 2


def feed_forward(nc, tag, x_in, x_out, weights, bp, b2, gamma, beta, before):
    n = x_in.shape[0] // GROUP

    with ExitStack() as es:
        def sb(name, shape, dt):
            return es.enter_context(nc.sbuf_tensor(tag + name, shape, dt))

        def bank(name, banks=1):
            return es.enter_context(nc.psum_tensor(tag + name, [P, banks * 512], F32))

        def sem(name):
            return es.enter_context(nc.semaphore(tag + name))

        wp_hi = sb("wp_hi", [P, KT, 2 * FF], F32R)
        wp_lo = sb("wp_lo", [P, KT, 2 * FF], F32R)
        w2_hi = sb("w2_hi", [P, HT, DIM], F32R)
        w2_lo = sb("w2_lo", [P, HT, DIM], F32R)
        bp_c = sb("bp", [P, 2 * HT], F32)
        b2_row = sb("b2", [P, DIM], F32)
        gamma_c = sb("gamma", [P, KT], F32)
        beta_c = sb("beta", [P, KT], F32)
        ident = sb("ident", [P, P], F32)
        pause = sb("pause", [P, 1], F32)
        minus_half = sb("minus_half", [P, GT], F32)
        xt = sb("xt", [P, 2, GT, DIM], F32)
        xres = sb("xres", [P, GT, DIM], F32)
        xnorm = sb("xnorm", [P, GT, DIM], F32)
        yout = sb("yout", [P, GT, DIM], F32)
        stats = sb("stats", [P, GT, 6], F32)
        meanvar = sb("meanvar", [P, GT, 2], F32)
        var_eps = sb("var_eps", [P, GT], F32)
        rstd = sb("rstd", [P, GT], F32)
        h_t = sb("h_t", [P, KT, GTOK], F32)
        h_hi = sb("h_hi", [P, 2, KT, GTOK], F32R)
        h_lo = sb("h_lo", [P, 2, KT, GTOK], F32R)
        gelu = sb("gelu", [P, 2, GTOK], F32)
        gated = sb("gated", [P, 2, GTOK], F32)
        u_hi = sb("u_hi", [P, 2, GTOK], F32R)
        u_lo = sb("u_lo", [P, 2, GTOK], F32R)

        ps_gate = [bank("ps_gate0"), bank("ps_gate1")]
        ps_a = [bank("ps_a0"), bank("ps_a1")]
        ps_y = bank("ps_y", 2)
        ps_ht = bank("ps_ht", 2)

        consts_loaded = sem("consts_loaded")
        w_hi_ready = sem("w_hi_ready")
        w_ready = sem("w_ready")
        ident_made = sem("ident_made")
        half_made = sem("half_made")
        x_loaded = [sem("x_loaded0"), sem("x_loaded1")]
        y_stored = sem("y_stored")
        xres_ready = sem("xres_ready")
        stats_ready = sem("stats_ready")
        meanvar_ready = sem("meanvar_ready")
        var_ready = sem("var_ready")
        rstd_ready = sem("rstd_ready")
        xnorm_ready = sem("xnorm_ready")
        h_transposed = sem("h_transposed")
        h_t_ready = sem("h_t_ready")
        h_hi_ready = sem("h_hi_ready")
        h_ready = sem("h_ready")
        gate_done = sem("gate_done")
        a_done = sem("a_done")
        gelu_ready = sem("gelu_ready")
        gated_ready = sem("gated_ready")
        u_hi_ready = sem("u_hi_ready")
        u_ready = sem("u_ready")
        down_done = sem("down_done")
        y_added = sem("y_added")

        x_in = x_in.rearrange("(n s) q d -> n (s q) d", s=GROUP)
        x_out = x_out.rearrange("(n s) q d -> n (s q) d", s=GROUP)

        def rows(group):
            return group.rearrange("(t p) d -> p t d", p=P)

        def groups(eng, step):
            for j in range(HT):
                step(0, 0, j, FIRST)
            with nc.Fori(1, n - 1, 2, engines=[eng.engine], hint_back_edge=True) as b:
                for j in range(HT):
                    step(b, 1, j, LOOP)
                for j in range(HT):
                    step(b + 1, 0, j, LOOP)
            for j in range(HT):
                step(n - 1, 1, j, LAST)
            for j in range(DOWN):
                step(n, 0, j, DRAIN)

        block = es.enter_context(nc.Block())

        @block.sync
        def _(sp):
            def load(b, parity):
                if counts(c := b - 1):
                    sp.wait_ge(xnorm_ready, c)
                    sp.wait_ge(xres_ready, c)
                sp.dma_start(xt[:, parity], rows(x_in[b])).then_inc(x_loaded[parity], 16)

            def store(b):
                sp.wait_ge(y_added, 2 * (b + 1))
                sp.dma_start(rows(x_out[b]), yout[:]).then_inc(y_stored, 16)

            load(0, 0)
            sp.wait_ge(before, 16 * GROUP * n)
            load(1, 1)
            load(2, 0)
            with sp.Fori(1, n - 3, 2) as b:
                store(b - 1)
                load(b + 2, 1)
                store(b)
                load(b + 3, 0)
            store(n - 4)
            load(n - 1, 1)
            for b in range(n - 3, n):
                store(b)
            sp.wait_ge(y_stored, 16 * n)

        @block.gpsimd
        def _(pool):
            make_identity(nc, pool, ident, ident_made)
            pool.memset(minus_half[:], -0.5).then_inc(half_made, 1)
            pool.wait_ge(half_made, 1)

            def norm_power(b):
                pool.wait_ge(var_ready, b + 1)
                if counts(c := b):
                    pool.wait_ge(xnorm_ready, c)
                pool.tensor_tensor(rstd[:], var_eps[:], minus_half[:], ALU.pow).then_inc(rstd_ready, 1)

            def residual(b, parity):
                pool.wait_ge(x_loaded[parity], 8 * (b - parity) + 16)
                if counts(c := 2 * b):
                    pool.wait_ge(y_added, c)
                if counts(c := 16 * b):
                    pool.wait_ge(y_stored, c)
                bias = b2_row[:].unsqueeze(1).to_broadcast([P, GT, DIM])
                pool.tensor_tensor(xres[:], xt[:, parity], bias, ALU.add).then_inc(xres_ready, 1)

            norm_power(0)
            pool.wait_ge(consts_loaded, 64)
            residual(0, 0)
            norm_power(1)
            with pool.Fori(1, n - 1, 2) as b:
                for parity in (1, 0):
                    residual(b + 1 - parity, parity)
                    norm_power(b + 2 - parity)
            residual(n - 1, 1)

        @block.scalar
        def _(act):
            with nc.allow_non_contiguous_dma(reason="columns of 128 scales"):
                act.dma_start(gamma_c[:], gamma.rearrange("(k p) -> p k", p=P)).then_inc(consts_loaded, 16)
                act.dma_start(beta_c[:], beta.rearrange("(k p) -> p k", p=P)).then_inc(consts_loaded, 16)
                act.dma_start(bp_c[:], bp.rearrange("(k p) -> p k", p=P)).then_inc(consts_loaded, 16)
            act.dma_start(b2_row[:], b2.partition_broadcast(P)).then_inc(consts_loaded, 16)
            act.wait_ge(weights.loaded["wp"], 16)
            for cols in WP_PARTS:
                act.activation(wp_hi[:, :, cols], weights.raw_wp[:, :, cols], ACT.Copy).then_inc(w_hi_ready, 1)
            act.wait_ge(weights.loaded["w2"], 16)
            act.activation(w2_hi[:], weights.raw_w2, ACT.Copy).then_inc(w_hi_ready, 1)
            act.wait_ge(consts_loaded, 64)

            def step(b, parity, j, part):
                if part == DRAIN:
                    return
                i = HT * b + j
                slot = j % 2
                act.wait_ge(gate_done, i + 1)
                if counts(c := i - 1):
                    act.wait_ge(gated_ready, c)
                act.activation(gelu[:, slot], ps_gate[slot][:], ACT.Gelu,
                               bias=bp_c[:, HT + j:HT + j + 1]).then_inc(gelu_ready, 1)
                act.wait_ge(gated_ready, i + 1)
                if counts(c := i - 1):
                    act.wait_ge(down_done, c)
                act.activation(u_hi[:, slot], gated[:, slot], ACT.Copy).then_inc(u_hi_ready, 1)

            groups(act, step)

        @block.vector
        def _(dve):
            def norm_stats(b, parity):
                dve.wait_ge(x_loaded[parity], 8 * (b - parity) + 16)
                for t in range(GT):
                    nc.vector.bn_stats(stats[:, t], xt[:, parity, t]).then_inc(stats_ready, 1)
                dve.wait_ge(stats_ready, GT * (b + 1))
                nc.vector.memset(pause[:], 0.0)
                for t in range(GT):
                    nc.vector.bn_aggr(meanvar[:, t], stats[:, t]).then_inc(meanvar_ready, 1)
                dve.wait_ge(meanvar_ready, GT * (b + 1))
                nc.vector.tensor_scalar(var_eps[:], meanvar[:, :, 1], EPS, None, ALU.add).then_inc(var_ready, 1)

            def norm_apply(b, parity):
                dve.wait_ge(rstd_ready, b + 1)
                if counts(c := b):
                    dve.wait_ge(h_transposed, c)
                for t in range(GT):
                    last = nc.vector.tensor_scalar(xnorm[:, t], xt[:, parity, t], meanvar[:, t, 0:1], rstd[:, t:t + 1],
                                                   ALU.subtract, ALU.mult)
                last.then_inc(xnorm_ready, 1)

            def scale_shift(b):
                dve.wait_ge(h_transposed, b + 1)
                for k in range(KT):
                    last = nc.vector.tensor_scalar(h_t[:, k], ps_ht[:, k * GTOK:(k + 1) * GTOK], gamma_c[:, k:k + 1],
                                                   beta_c[:, k:k + 1], ALU.mult, ALU.add)
                last.then_inc(h_t_ready, 1)

            def split_h(b, parity):
                dve.wait_ge(h_t_ready, b + 1)
                if counts(c := HT * (b - 1)):
                    dve.wait_ge(a_done, c)
                nc.vector.tensor_copy(h_hi[:, parity], h_t[:]).then_inc(h_hi_ready, 1)
                dve.wait_ge(h_hi_ready, b + 1)
                nc.vector.tensor_tensor(h_lo[:, parity], h_t[:], h_hi[:, parity].bitcast(F32),
                                        ALU.subtract).then_inc(h_ready, 1)

            norm_stats(0, 0)
            norm_apply(0, 0)
            for i, cols in enumerate(WP_PARTS):
                if i == 2:
                    dve.wait_ge(consts_loaded, 64)
                    scale_shift(0)
                    split_h(0, 0)
                dve.wait_ge(w_hi_ready, i + 1)
                nc.vector.tensor_tensor(wp_lo[:, :, cols], weights.raw_wp[:, :, cols], wp_hi[:, :, cols].bitcast(F32),
                                        ALU.subtract).then_inc(w_ready, 1)
            dve.wait_ge(w_hi_ready, len(WP_PARTS) + 1)
            nc.vector.tensor_tensor(w2_lo[:], weights.raw_w2, w2_hi[:].bitcast(F32), ALU.subtract).then_inc(w_ready, 1)

            def step(b, parity, j, part):
                i = HT * b + j
                slot = j % 2
                if part != DRAIN:
                    dve.wait_ge(a_done, i + 1)
                    dve.wait_ge(gelu_ready, i + 1)
                    if counts(c := i - 1):
                        dve.wait_ge(u_ready, c)
                    nc.vector.scalar_tensor_tensor(gated[:, slot], ps_a[slot][:], bp_c[:, j:j + 1], gelu[:, slot],
                                                   ALU.add, ALU.mult).then_inc(gated_ready, 1)
                if j == DOWN - 1 and part != FIRST:
                    dve.wait_ge(down_done, HT * b)
                    dve.wait_ge(xres_ready, b)
                    for half in range(2):
                        r = slice(half * TT, (half + 1) * TT)
                        nc.vector.tensor_tensor(yout[:, r].rearrange("p t d -> p (t d)"),
                                                ps_y[:, half * 512:(half + 1) * 512],
                                                xres[:, r].rearrange("p t d -> p (t d)"),
                                                ALU.add).then_inc(y_added, 1)
                if part != DRAIN:
                    dve.wait_ge(u_hi_ready, i + 1)
                    if counts(c := i - 1):
                        dve.wait_ge(down_done, c)
                    nc.vector.tensor_tensor(u_lo[:, slot], gated[:, slot], u_hi[:, slot].bitcast(F32),
                                            ALU.subtract).then_inc(u_ready, 1)
                if part in (FIRST, LOOP):
                    if j == 2:
                        norm_stats(b + 1, 1 - parity)
                    if j == 3:
                        norm_apply(b + 1, 1 - parity)
                    if j == 5:
                        scale_shift(b + 1)
                    if j == 6:
                        split_h(b + 1, 1 - parity)

            groups(dve, step)

        @block.tensor
        def _(pe):
            def transpose_h(b):
                pe.wait_ge(xnorm_ready, b + 1)
                if counts(c := b):
                    pe.wait_ge(h_t_ready, c)
                for k in range(KT):
                    for t in range(GT):
                        last = nc.tensor.transpose(ps_ht[:, k * GTOK + t * P:k * GTOK + (t + 1) * P],
                                                   xnorm[:, t, k * P:(k + 1) * P], ident[:])
                last.then_inc(h_transposed, 1)

            def up(out, column, parity, done):
                passes = [t for k in range(KT) for t in ((wp_hi, h_hi, k), (wp_hi, h_lo, k), (wp_lo, h_hi, k))]
                for i, (w, h, k) in enumerate(passes):
                    last = nc.tensor.matmul(out, w[:, k, column:column + P], h[:, parity, k], start=i == 0, stop=i == 5)
                last.then_inc(done, 1)

            def step(b, parity, j, part):
                i = HT * b + j
                slot = j % 2
                if part != DRAIN:
                    pe.wait_ge(h_ready, b + 1)
                    if part == FIRST and j % 4 == 0:
                        pe.wait_ge(w_ready, 2 * (j // 4 + 1))
                    if counts(c := i - 1):
                        pe.wait_ge(gelu_ready, c)
                    up(ps_gate[slot][:], FF + j * P, parity, gate_done)
                    if counts(c := i - 1):
                        pe.wait_ge(gated_ready, c)
                    up(ps_a[slot][:], j * P, parity, a_done)
                if alive(part, j, DOWN):
                    q = (j - DOWN) % HT
                    pe.wait_ge(u_ready, i - DOWN + 1)
                    if part == FIRST and q == 0:
                        pe.wait_ge(w_ready, len(WP_PARTS) + 1)
                    if q == 0:
                        if counts(c := 2 * b):
                            pe.wait_ge(y_added, c)
                    for t in range(GT):
                        for s, (a, m) in enumerate(((u_hi, w2_hi), (u_lo, w2_hi), (u_hi, w2_lo))):
                            last = nc.tensor.matmul(ps_y[:, t * DIM:(t + 1) * DIM], a[:, q % 2, t * P:(t + 1) * P],
                                                    m[:, q], start=q == 0 and t % 2 == 0 and s == 0,
                                                    stop=q == HT - 1 and t % 2 == 1 and s == 2,
                                                    skip_group_check=True)
                    last.then_inc(down_done, 1)
                if part in (FIRST, LOOP) and j == 4:
                    transpose_h(b + 1)

            pe.wait_ge(ident_made, 2)
            transpose_h(0)
            groups(pe, step)


_W = "L0_xattn_"
_INS = ["x", "ctx_768"] + [_W + w for w in (
    "Wq1", "Wk1", "Wv1", "Wo1", "bo1", "Wq2", "Wk2", "Wv2", "Wo2", "bo2", "Wp", "bp", "W2", "b2",
    "g1", "be1", "g2", "be2", "g3", "be3")]


def block_program(nc, a, out):
    x1 = nc.dram_tensor("after_self_attention", a["x"].shape, F32).ap()
    x2 = nc.dram_tensor("after_cross_attention", a["x"].shape, F32).ap()
    w = {k[len(_W):]: v for k, v in a.items() if k.startswith(_W)}
    with ExitStack() as es:
        raw = [es.enter_context(nc.sbuf_tensor(f"raw{i}", [P, len(WEIGHTS) * W_COLS], F32)) for i in range(2)]

        def loaded(tag, names):
            return {k: es.enter_context(nc.semaphore(f"{tag}loaded_{k}")) for k in names}

        self_w = AttentionWeights(raw[0], loaded("self_", WEIGHTS), [w[k] for k in ("Wq1", "Wk1", "Wv1", "Wo1")], False)
        cross_w = AttentionWeights(raw[1], loaded("cross_", WEIGHTS), [w[k] for k in ("Wq2", "Wk2", "Wv2", "Wo2")], True)
        ff_w = FeedForwardWeights(raw[0], loaded("ff_", ("wp", "w2")), w["Wp"], w["W2"])
        yout = [es.enter_context(nc.sbuf_tensor(f"yout{i}", [P, TT, DIM], F32)) for i in range(2)]
        stored = [es.enter_context(nc.semaphore(tag + "y_stored")) for tag in ("self_", "cross_")]
        attention(nc, "self_", a["x"], None, x1, self_w, w["bo1"], w["g1"], w["be1"], cross_w.load,
                  yout[0], stored[0], None)
        attention(nc, "cross_", x1, a["ctx_768"], x2, cross_w, w["bo2"], w["g2"], w["be2"], ff_w.load,
                  yout[1], stored[1], stored[0])
        feed_forward(nc, "ff_", x2, out, ff_w, w["bp"], w["b2"], w["g3"], w["be3"], stored[1])


def kernel(**inputs):
    import numpy as np
    import concourse.bacc as bacc
    from concourse.bass_utils import run_bass_kernel_spmd

    nc = bacc.Bacc("TRN2", target_bir_lowering=False, num_devices=1)
    arrays, aps = {}, {}
    for name in _INS:
        arrays["in_" + name] = np.ascontiguousarray(inputs[name])
        aps[name] = nc.dram_tensor("in_" + name, arrays["in_" + name].shape, F32, kind="ExternalInput").ap()
    out = nc.dram_tensor("out", arrays["in_x"].shape, F32, kind="ExternalOutput").ap()
    block_program(nc, aps, out)
    r = run_bass_kernel_spmd(nc, [arrays], core_ids=[0])
    return r.results[0]["out"]
```
